# Optimizing a Trainium2 kernel written in Bass

```python
import numpy as np
import jax
import jax.numpy as jnp

def _softmax(x, axis=-1):
    return jax.nn.softmax(x, axis=axis)

def _gelu(x):
    return jax.nn.gelu(x, approximate=True)

def _silu(x):
    return jax.nn.silu(x)

def _sigmoid(x):
    return jax.nn.sigmoid(x)

def _layernorm(x, axis=-1, eps=1e-05):
    m = jnp.mean(x, axis=axis, keepdims=True)
    v = jnp.var(x, axis=axis, keepdims=True)
    return (x - m) / jnp.sqrt(v + eps)

def _scatter_add(tgt, idx, src, axis=0):
    return tgt.at[idx].add(src)

def _segment_sum(src, seg, n):
    return jax.ops.segment_sum(src, seg, n)
kernel_name = 'mk_adj_preln_d1_adj_r2_296aba'

def setup_inputs(seed: int=0):
    np.random.seed(seed)
    _w = jnp.asarray

    def _rec_inputs():
        import jax
        import jax.numpy as jnp
        _gk = jax.random.key(seed)
        x = -0.0001538 + 1 * jax.random.normal(jax.random.fold_in(_gk, 1), (128, 128, 384), jnp.float32)
        _a = jax.random.bernoulli(jax.random.fold_in(_gk, 2), 0.0625, (128, 128, 128))
        _a = jnp.logical_or(_a, jnp.eye(128, dtype=bool))
        adj = _a
        return (x, adj)
    x, adj = _rec_inputs()

    def _L0_gnn_setup():
        import jax, jax.numpy as jnp
        import numpy as np
        B, S, H = (4, 1024, 384)
        NUM_HEADS = 6
        HEAD_SIZE = H // NUM_HEADS
        NEG = -9000000000000000.0

        def _heads(x):
            b, s, _ = x.shape
            return x.reshape(b, s, NUM_HEADS, HEAD_SIZE).transpose(0, 2, 1, 3)
        key = jax.random.key(seed)
        ks = jax.random.split(key, 10)
        seq_inputs = jax.random.normal(ks[0], (B, S, H), dtype=jnp.float32)
        gm = jax.random.randint(ks[1], (B, S, S), 0, 2) > 0
        graph_mask = gm | jnp.eye(S, dtype=bool)[None]
        sc = 1.0 / np.sqrt(H)
        Wq = jax.random.normal(ks[2], (H, H), dtype=jnp.float32) * sc
        bq = jnp.zeros((H,), dtype=jnp.float32)
        Wk = jax.random.normal(ks[3], (H, H), dtype=jnp.float32) * sc
        bk = jnp.zeros((H,), dtype=jnp.float32)
        Wv = jax.random.normal(ks[4], (H, H), dtype=jnp.float32) * sc
        bv = jnp.zeros((H,), dtype=jnp.float32)
        Wf = jax.random.normal(ks[5], (H, H), dtype=jnp.float32) * sc
        bf = jnp.zeros((H,), dtype=jnp.float32)
        return {'seq_inputs': seq_inputs, 'Wq': Wq, 'bq': bq, 'Wk': Wk, 'bk': bk, 'Wv': Wv, 'bv': bv, 'Wf': Wf, 'bf': bf, 'graph_mask': graph_mask}
    _L0_gnn_all = _L0_gnn_setup()
    _L0_gnn_in = {k: v for k, v in _L0_gnn_all.items() if k in ('Wq', 'bq', 'Wk', 'bk', 'Wv', 'bv', 'Wf', 'bf')}
    del _L0_gnn_all
    return {'x': x, 'adj': adj, 'L0_gnn_Wq': _L0_gnn_in['Wq'], 'L0_gnn_bq': _L0_gnn_in['bq'], 'L0_gnn_Wk': _L0_gnn_in['Wk'], 'L0_gnn_bk': _L0_gnn_in['bk'], 'L0_gnn_Wv': _L0_gnn_in['Wv'], 'L0_gnn_bv': _L0_gnn_in['bv'], 'L0_gnn_Wf': _L0_gnn_in['Wf'], 'L0_gnn_bf': _L0_gnn_in['bf']}

def reference(x, adj, L0_gnn_Wq, L0_gnn_bq, L0_gnn_Wk, L0_gnn_bk, L0_gnn_Wv, L0_gnn_bv, L0_gnn_Wf, L0_gnn_bf):
    import jax
    import jax.numpy as jnp

    def _L0_gnn_ref(seq_inputs, Wq, bq, Wk, bk, Wv, bv, Wf, bf, graph_mask):
        import jax, jax.numpy as jnp
        import numpy as np
        B, S, H = (4, 1024, 384)
        NUM_HEADS = 6
        HEAD_SIZE = H // NUM_HEADS
        NEG = -9000000000000000.0

        def _heads(x):
            b, s, _ = x.shape
            return x.reshape(b, s, NUM_HEADS, HEAD_SIZE).transpose(0, 2, 1, 3)
        q = _heads(seq_inputs @ Wq + bq)
        k = _heads(seq_inputs @ Wk + bk)
        v = _heads(seq_inputs @ Wv + bv)
        scores = jnp.einsum('bhqd,bhkd->bhqk', q, k) / np.sqrt(HEAD_SIZE)
        bias = jnp.where(graph_mask, 0.0, NEG)[:, None]
        probs = jax.nn.softmax(scores + bias, axis=-1)
        ctx = jnp.einsum('bhqk,bhkd->bhqd', probs, v)
        ctx = ctx.transpose(0, 2, 1, 3).reshape(seq_inputs.shape[0], seq_inputs.shape[1], H)
        return ctx @ Wf + bf
    h = jnp.maximum(_layernorm(x, axis=-1), 0.0)
    x = x + _L0_gnn_ref(h, L0_gnn_Wq, L0_gnn_bq, L0_gnn_Wk, L0_gnn_bk, L0_gnn_Wv, L0_gnn_bv, L0_gnn_Wf, L0_gnn_bf, adj)
    return x

_drawn_inputs = setup_inputs


def setup_inputs(seed=0):
    import zlib

    import numpy as np

    out = dict(_drawn_inputs(seed))
    spreads = {'L0_gnn_bq': (0.0, 0.788),
     'L0_gnn_bk': (0.0, 0.8),
     'L0_gnn_bv': (0.0, 0.1),
     'L0_gnn_bf': (0.0, 0.1)}
    factors = {}
    for name, (base, spread) in spreads.items():
        noise = np.random.default_rng([zlib.crc32(name.encode()), seed]).standard_normal(out[name].shape)
        drawn = base * np.exp(spread * noise) if base else spread * noise
        out[name] = jnp.asarray(drawn.astype(out[name].dtype))
    for name, factor in factors.items():
        out[name] = (out[name] * factor).astype(out[name].dtype)
    return out
```

```python
import concourse.bass as bass
from concourse import mybir

F32 = mybir.dt.float32
F16 = mybir.dt.float16
U8 = mybir.dt.uint8
U32 = mybir.dt.uint32
ALU = mybir.AluOpType
ACT = mybir.ActivationFunctionType
AX = mybir.AxisListType

P = 128
HEADS = 6
DH = 64
EPS = 1e-5
NEG = -9000000000000000.0

H_SCALE = 2.0 ** 11
PROJ_SCALE = 2.0 ** -19
QKV_EXP = -8
PROB_SCALE = 2.0 ** 15
W_TARGET = 2.0 ** 13
W_FLOOR = 2.0 ** -26

UNROLL = 8
LAST_LAG = 3
LEAD = 6


def ring(b, n):
    return b % n


class Step:

    def __init__(self, base, off):
        self.base, self.off = base, off

    def batch(self, lag):
        return Batch(self.base, self.off + lag)


class Batch:
    def __init__(self, base, off):
        self.base, self.off = base, off

    def exists(self, batches):
        return not isinstance(self.base, int) or 0 <= self.base + self.off < batches

    def count(self, per=1, plus=0):
        return self.base * per + (self.off * per + plus)

    def dma_count(self, n, per, plus=0):
        if isinstance(self.base, int):
            return (self.base + self.off) // n * per + plus
        return self.base * (per // n) + (self.off // n * per + plus)


def wait(eng, sem, value):
    if not isinstance(value, int) or value > 0:
        eng.wait_ge(sem, value)


def apart(eng):
    eng.nop(nofuse=True)


def slots(eng, batches, body):
    first = -LEAD
    for t in range(first, UNROLL):
        body(Step(0, t))
    with eng.Fori(1, batches // UNROLL - 1) as n:
        for off in range(UNROLL):
            body(Step(n * UNROLL, off))
    for off in range(UNROLL + LAST_LAG):
        body(Step(batches - UNROLL, off))


def graph_attention(nc, x, adj, Wq, bq, Wk, bk, Wv, bv, Wf, bf, out):
    batches, tokens, hidden = x.shape
    assert tokens == P and hidden == HEADS * DH and batches % UNROLL == 0
    KT = hidden // P
    PAIRS = HEADS // 2
    assert PAIRS == KT

    from contextlib import ExitStack
    with ExitStack() as ctx:
        def sb(name, shape, dt=F32):
            return ctx.enter_context(nc.sbuf_tensor(name, shape, dt))

        def bank(name):
            return ctx.enter_context(nc.psum_tensor(name, [P, 512], F32))

        def sem(name):
            return ctx.enter_context(nc.semaphore(name))

        ident = sb("ident", [P, P])
        ones_row = sb("ones_row", [1, P])
        w_raw = [sb(f"w_raw_{n}", [P, KT, hidden]) for n in "qkvf"]
        w_hi = [sb(f"w_hi_{n}", [P, KT, hidden], F16) for n in "qkvf"]
        w_lo = [sb(f"w_lo_{n}", [P, KT, hidden], F16) for n in "qkvf"]
        extremes = sb("extremes", [P, 10])
        ext_all = sb("ext_all", [P, 10])
        bias_max = sb("bias_max", [P, 2])
        top = sb("top", [P, 4])
        top_pow = sb("top_pow", [P, 4])
        top_rec = sb("top_rec", [P, 4])
        w_scale = sb("w_scale", [P, 4])
        pair_pow = sb("pair_pow", [P, 2])
        pair_scale = sb("pair_scale", [P, 1])
        score_scale = sb("score_scale", [P, 1])
        out_scale = sb("out_scale", [P, 1])
        mask_scale = sb("mask_scale", [P, 2])
        qk_bias = sb("qk_bias", [P, 2, KT])
        bv_col = sb("bv_col", [P, KT])
        bv_rep = sb("bv_rep", [P, KT, P])
        bf_row = sb("bf_row", [1, hidden])
        out_bias = sb("out_bias", [P, hidden])

        X_RING, XN, IO = 8, 2, 4
        x_sb = sb("x_sb", [P, X_RING, hidden])
        adj_sb = sb("adj_sb", [P, X_RING, P], U8)
        stats = sb("stats", [P, 2, 6])
        mean_var = sb("mean_var", [P, 2, 2])
        var_eps = sb("var_eps", [P, 2, 1])
        neg_mean = sb("neg_mean", [P, 2, 1])
        rstd = sb("rstd", [P, 2, 1])
        half_power = sb("half_power", [P, 1])
        xn = sb("xn", [P, XN, hidden])
        hT_hi = sb("hT_hi", [P, 2, KT, 2 * P], F16)
        hT_lo = sb("hT_lo", [P, 2, KT, 2 * P], F16)
        qk_full = sb("qk_full", [P, 2, KT, 2 * P])
        qk_hi = sb("qk_hi", [P, 2, 2, KT, 2 * P], F16)
        qk_lo = sb("qk_lo", [P, 2, 2, KT, 2 * P], F16)
        v_hi = sb("v_hi", [P, X_RING, hidden], F16)
        v_lo = sb("v_lo", [P, X_RING, hidden], F16)
        mask = sb("mask", [P, 2, P])
        neg_scores = sb("neg_scores", [P, 2, HEADS, P])
        neg_max = sb("neg_max", [P, 2, HEADS])
        probs = sb("probs", [P, 2, HEADS, P])
        sums = sb("sums", [P, 2, HEADS])
        inv_sums = sb("inv_sums", [P, 2, HEADS])
        probs_n = sb("probs_n", [P, 2, HEADS, P])
        pT_hi = sb("pT_hi", [P, 2, HEADS, P], F16)
        pT_lo = sb("pT_lo", [P, 2, HEADS, P], F16)
        ctx_hi = sb("ctx_hi", [P, 2, KT, P], F16)
        ctx_lo = sb("ctx_lo", [P, 2, KT, P], F16)
        out_sb = sb("out_sb", [P, IO, hidden])

        score_ps = ctx.enter_context(nc.psum_tensor("score_ps", [P, 2, 512], F32))
        pT_ps = ctx.enter_context(nc.psum_tensor("pT_ps", [P, 2, 512], F32))
        ctx_ps = bank("ctx_ps")
        io_ps = bank("io_ps")
        proj_ps = [bank("proj_ps0"), bank("proj_ps1")]

        consts_loaded = sem("consts_loaded")
        w_loaded = [sem(f"w_loaded_{n}") for n in "qkvf"]
        loaded = [sem(f"loaded{i}") for i in range(IO)]
        stored = [sem(f"stored{i}") for i in range(IO)]
        ident_ready = sem("ident_ready")
        ext_ready = sem("ext_ready")
        ext_reduced = sem("ext_reduced")
        setup_step = sem("setup_step")
        w_hi_ready = sem("w_hi_ready")
        w_lo_ready = sem("w_lo_ready")
        bias_summed = sem("bias_summed")
        bias_ready = sem("bias_ready")
        stats_done = sem("stats_done")
        ln_step = sem("ln_step")
        xn_ready = sem("xn_ready")
        resid_ready = sem("resid_ready")
        hT_done = sem("hT_done")
        hT_hi_ready = sem("hT_hi_ready")
        hT_split = sem("hT_split")
        proj_done = sem("proj_done")
        proj_out = sem("proj_out")
        qk_hi_ready = sem("qk_hi_ready")
        qk_split = sem("qk_split")
        v_done = sem("v_done")
        v_hi_ready = sem("v_hi_ready")
        v_split = sem("v_split")
        mask_ready = sem("mask_ready")
        scores_done = sem("scores_done")
        masked = sem("masked")
        exp_done = sem("exp_done")
        inverted = sem("inverted")
        normed = sem("normed")
        pT_done = sem("pT_done")
        pT_hi_ready = sem("pT_hi_ready")
        pT_split = sem("pT_split")
        ctx_done = sem("ctx_done")
        ctx_hi_ready = sem("ctx_hi_ready")
        ctx_split = sem("ctx_split")
        out_done = sem("out_done")
        out_ready = sem("out_ready")

        block = ctx.enter_context(nc.Block())

        def pair_of(b):
            o = b.off
            return o // 2 % 2, slice(o % 2 * P, (o % 2 + 1) * P)

        def next_pair(t):
            b = Batch(t.base, t.off // 2 * 2 + 2)
            return b.off // 2 % 2, b

        @block.sync
        def _(sp):
            def load(b):
                i = ring(b.off, X_RING)
                wait(sp, out_ready, b.count(plus=1 - X_RING))
                apart(sp)
                wait(sp, mask_ready, b.count(plus=1 - X_RING))
                apart(sp)
                wait(sp, xn_ready, b.count(plus=1 - IO))
                apart(sp)
                got = loaded[ring(b.off, IO)]
                if isinstance(b.base, int):
                    src_x, src_adj = x[b.base + b.off], adj[b.base + b.off]
                else:
                    n = b.base + b.off
                    src_x = x[bass.ds(n, 1)].rearrange("o p h -> (o p) h")
                    src_adj = adj[bass.ds(n, 1)].rearrange("o p h -> (o p) h")
                sp.dma_start(x_sb[:, i, :], src_x).then_inc(got, 16)
                sp.dma_start(adj_sb[:, i, :], src_adj).then_inc(got, 16)

            def store(b):
                wait(sp, out_ready, b.count(plus=1))
                apart(sp)
                if isinstance(b.base, int):
                    dst = out[b.base + b.off]
                else:
                    dst = out[bass.ds(b.base + b.off, 1)].rearrange("o p h -> (o p) h")
                sp.dma_start(dst, out_sb[:, ring(b.off, IO), :]).then_inc(stored[ring(b.off, IO)], 16)

            sp.dma_start(w_raw[0][:, :, :], Wq.rearrange("(t p) n -> p t n", p=P)).then_inc(w_loaded[0], 16)
            sp.dma_start(w_raw[1][:, :, :], Wk.rearrange("(t p) n -> p t n", p=P)).then_inc(w_loaded[1], 16)
            sp.dma_start(w_raw[2][:, :, :], Wv.rearrange("(t p) n -> p t n", p=P)).then_inc(w_loaded[2], 16)
            sp.dma_start(w_raw[3][:, :, :], Wf.rearrange("(t p) n -> p t n", p=P)).then_inc(w_loaded[3], 16)
            sp.dma_start(extremes[:, 4:7], bq.rearrange("(t p) -> p t", p=P), allow_slow_non_contiguous=True).then_inc(consts_loaded, 16)
            sp.dma_start(extremes[:, 7:10], bk.rearrange("(t p) -> p t", p=P), allow_slow_non_contiguous=True).then_inc(consts_loaded, 16)
            sp.dma_start(bv_col[:, :], bv.rearrange("(t p) -> p t", p=P), allow_slow_non_contiguous=True).then_inc(consts_loaded, 16)
            sp.dma_start(bf_row[:, :], bf.rearrange("(o n) -> o n", o=1)).then_inc(consts_loaded, 16)

            def slot(t):
                b = t.batch(6)
                if b.exists(batches):
                    load(b)
                b = t.batch(-2)
                if b.exists(batches):
                    store(b)

            slots(sp, batches, slot)
            for i in range(IO):
                sp.wait_ge(stored[i], 16 * (batches // IO))

        @block.gpsimd
        def _(pool):
            pool.memset(ident[:, :], 0.0).then_inc(ident_ready, 1)
            pool.memset(ones_row[:, :], 1.0).then_inc(ident_ready, 1)
            pool.memset(half_power[:, :], -0.5).then_inc(ident_ready, 1)
            pool.wait_ge(ident_ready, 3)
            pool.affine_select(out=ident[:, :], in_=ident[:, :], compare_op=ALU.not_equal, fill=1.0, base=0,
                               pattern=[[-1, P]], channel_multiplier=1).then_inc(ident_ready, 1)
            pool.wait_ge(ext_ready, 4)
            pool.wait_ge(consts_loaded, 64)
            pool.partition_all_reduce(ext_all[:, :], extremes[:, :], P, bass.bass_isa.ReduceOp.absmax)\
                .then_inc(ext_reduced, 1)

            def make_mask(b):
                wait(pool, masked, b.count(per=HEADS, plus=-HEADS))
                if isinstance(b.base, int) and b.base + b.off == 0:
                    pool.wait_ge(setup_step, 9)
                apart(pool)
                pool.tensor_scalar(mask[:, ring(b.off, 2), :], adj_sb[:, ring(b.off, X_RING), :],
                                   mask_scale[:, 0:1], mask_scale[:, 1:2], ALU.mult, ALU.add)\
                    .then_inc(mask_ready, 1)

            def layer_norm(b):
                s = ring(b.off, 2)
                xb = x_sb[:, ring(b.off, X_RING), :]
                wait(pool, loaded[ring(b.off, IO)], b.dma_count(IO, 32, 32))
                wait(pool, stats_done, b.count(per=2, plus=2))
                apart(pool)
                pool.tensor_scalar(var_eps[:, s, :], mean_var[:, s, 1:2], EPS, H_SCALE ** -2, ALU.add, ALU.mult)\
                    .then_inc(ln_step, 1)
                pool.tensor_scalar(neg_mean[:, s, :], mean_var[:, s, 0:1], -1.0, 0.0, ALU.mult, ALU.add)\
                    .then_inc(ln_step, 1)
                wait(pool, ln_step, b.count(per=3, plus=2))
                pool.tensor_tensor(rstd[:, s, :], var_eps[:, s, :], half_power[:, :], ALU.pow).then_inc(ln_step, 1)
                wait(pool, ln_step, b.count(per=3, plus=3))
                wait(pool, hT_done, b.count(plus=-1))
                apart(pool)
                pool.tensor_scalar(xn[:, ring(b.off, XN), :], xb, neg_mean[:, s, :], rstd[:, s, :],
                                   ALU.add, ALU.mult).then_inc(xn_ready, 1)
                if isinstance(b.base, int) and b.base + b.off == 0:
                    pool.wait_ge(bias_ready, 1)
                wait(pool, xn_ready, b.count(plus=1))
                pool.tensor_tensor(xb, xb, out_bias[:, :], ALU.add).then_inc(resid_ready, 1)

            def qk_low(t):
                g, first = next_pair(t)
                c = t.off % 2
                wait(pool, qk_hi_ready, t.batch(2).count(plus=1))
                wait(pool, scores_done, first.count(plus=-2))
                pool.tensor_tensor(qk_lo[:, g, c, :, :], qk_full[:, c, :, :], qk_hi[:, g, c, :, :], ALU.subtract)\
                    .then_inc(qk_split, 1)

            def normalise(b):
                s = ring(b.off, 2)
                wait(pool, exp_done, b.count(per=HEADS, plus=HEADS))
                wait(pool, inverted, b.count(plus=1))
                wait(pool, pT_done, b.count(plus=-1))
                pool.tensor_tensor(probs_n[:, s, :, :], probs[:, s, :, :],
                                   inv_sums[:, s, :].unsqueeze(2).to_broadcast([P, HEADS, P]), ALU.mult)\
                    .then_inc(normed, 1)

            def slot(t):
                b = t.batch(-1)
                if b.exists(batches):
                    normalise(b)
                b = t.batch(1)
                if b.exists(batches):
                    make_mask(b)
                b = t.batch(5)
                if b.exists(batches):
                    layer_norm(b)
                if t.batch(2).exists(batches):
                    qk_low(t)

            slots(pool, batches, slot)

        @block.scalar
        def _(act):
            act.wait_ge(setup_step, 5)
            for n in range(4):
                act.wait_ge(w_loaded[n], 16)
                act.activation(w_hi[n][:, :, :], w_raw[n][:, :, :], ACT.Copy, scale=w_scale[:, n:n + 1])\
                    .then_inc(w_hi_ready, 1)

            def qk_out(t, j):
                c = t.off % 2
                b = t.batch(2)
                wait(act, proj_done, b.count(per=KT, plus=j + 1))
                if j == 0:
                    wait(act, qk_split, b.count(plus=-1))
                    if isinstance(t.base, int) and b.base + b.off == 0:
                        act.wait_ge(setup_step, 11)
                act.activation(qk_full[:, c, j, :], proj_ps[j % 2][:, 0:2 * P], ACT.Identity,
                               bias=qk_bias[:, c, j:j + 1], scale=PROJ_SCALE).then_inc(proj_out, 1)

            def exps(b, heads):
                s = ring(b.off, 2)
                for h in heads:
                    if h == 0:
                        wait(act, normed, b.count(plus=-1))
                    wait(act, masked, b.count(per=HEADS, plus=h + 1))
                    act.activation(probs[:, s, h, :], neg_scores[:, s, h, :], ACT.Exp, scale=-1.0,
                                   bias=neg_max[:, s, h:h + 1], accum_out=sums[:, s, h:h + 1])\
                        .then_inc(exp_done, 1)

            def ctx_high(b):
                wait(act, ctx_done, b.count(plus=1))
                wait(act, out_done, b.count(plus=-1))
                act.activation(ctx_hi[:, ring(b.off, 2), :, :], ctx_ps[:, 0:hidden].rearrange("p (j q) -> p j q", j=KT),
                               ACT.Copy, scale=1.0 / PROB_SCALE).then_inc(ctx_hi_ready, 1)

            def pT_high(b):
                wait(act, pT_done, b.count(plus=1))
                wait(act, ctx_done, b.count(plus=-1))
                act.activation(pT_hi[:, ring(b.off, 2), :, :].rearrange("p (r j) q -> p r (j q)", r=2),
                               pT_ps[:, :, 0:hidden], ACT.Copy, scale=PROB_SCALE).then_inc(pT_hi_ready, 1)

            def v_high(b):
                wait(act, v_done, b.count(plus=1))
                wait(act, ctx_done, b.count(plus=1 - X_RING))
                act.activation(v_hi[:, ring(b.off, X_RING), :], proj_ps[1][:, 0:hidden], ACT.Copy,
                               scale=PROJ_SCALE).then_inc(v_hi_ready, 1)

            def hT_high(b):
                g, cols = pair_of(b)
                wait(act, hT_done, b.count(plus=1))
                wait(act, v_done, Batch(b.base, b.off // 2 * 2).count(plus=-2))
                act.activation(hT_hi[:, g, :, cols], io_ps[:, 0:hidden].rearrange("p (j q) -> p j q", j=KT),
                               ACT.Relu).then_inc(hT_hi_ready, 1)

            def slot(t):
                scored, used = t.batch(0), t.batch(-2)
                projecting = t.batch(2).exists(batches)
                if projecting:
                    qk_out(t, 0)
                if scored.exists(batches):
                    exps(scored, range(0, PAIRS))
                if used.exists(batches):
                    ctx_high(used)
                if scored.exists(batches):
                    exps(scored, range(PAIRS, HEADS))
                if projecting:
                    qk_out(t, 1)
                    qk_out(t, 2)
                b = t.batch(-1)
                if b.exists(batches):
                    pT_high(b)
                if projecting:
                    v_high(t.batch(2))
                b = t.batch(4)
                if b.exists(batches):
                    hT_high(b)

            slots(act, batches, slot)

        @block.vector
        def _(dve):
            for n in range(4):
                dve.wait_ge(w_loaded[n], 16)
                dve.tensor_reduce(extremes[:, n:n + 1], w_raw[n][:, :, :], AX.XY, ALU.max,
                                  apply_absolute_value=True).then_inc(ext_ready, 1)
            dve.wait_ge(consts_loaded, 64)
            for j in range(KT):
                last = dve.tensor_copy(bv_rep[:, j, :], bv_col[:, j:j + 1].to_broadcast([P, P]))
            last.then_inc(bias_ready, 1)
            dve.wait_ge(ext_reduced, 1)
            dve.tensor_reduce(bias_max[:, :], ext_all[:, 4:10].rearrange("p (c t) -> p c t", c=2), AX.X, ALU.max)\
                .then_inc(setup_step, 1)
            dve.tensor_scalar(top[:, 2:4], ext_all[:, 2:4], W_FLOOR, None, ALU.max).then_inc(setup_step, 1)
            dve.wait_ge(setup_step, 2)
            dve.scalar_tensor_tensor(out=top[:, 0:2], in0=bias_max[:, :], scalar=2.0 ** QKV_EXP, in1=ext_all[:, 0:2],
                                     op0=ALU.mult, op1=ALU.max).then_inc(setup_step, 1)
            dve.wait_ge(setup_step, 3)
            dve.tensor_scalar(top_rec[:, :], top[:, :], W_FLOOR, None, ALU.max).then_inc(ext_ready, 1)
            dve.wait_ge(ext_ready, 5)
            dve.tensor_scalar(top_pow[:, :].bitcast(U32), top_rec[:, :].bitcast(U32), 0x7f800000, None,
                              ALU.bitwise_and).then_inc(ext_ready, 1)
            dve.wait_ge(ext_ready, 6)
            dve.reciprocal(top_rec[:, :], top_pow[:, :]).then_inc(setup_step, 1)
            dve.wait_ge(setup_step, 4)
            dve.tensor_scalar(w_scale[:, :], top_rec[:, :], W_TARGET, None, ALU.mult).then_inc(setup_step, 1)
            dve.wait_ge(setup_step, 5)
            pows = top_pow[:, :].rearrange("p (c t) -> p c t", t=2)
            dve.tensor_tensor(pair_pow[:, :], pows[:, :, 0], pows[:, :, 1], ALU.mult).then_inc(setup_step, 1)
            dve.tensor_tensor(pair_scale[:, :], w_scale[:, 0:1], w_scale[:, 1:2], ALU.mult).then_inc(setup_step, 1)
            dve.wait_ge(setup_step, 7)
            dve.tensor_scalar(mask_scale[:, 0:1], pair_scale[:, :], -NEG * 8.0 * 2.0 ** (2 * QKV_EXP), None, ALU.mult)\
                .then_inc(setup_step, 1)
            dve.tensor_scalar(mask_scale[:, 1:2], pair_scale[:, :], NEG * 8.0 * 2.0 ** (2 * QKV_EXP), None, ALU.mult)\
                .then_inc(setup_step, 1)
            for c in range(2):
                dve.tensor_scalar(qk_bias[:, c, :], extremes[:, 4 + KT * c:4 + KT * (c + 1)], w_scale[:, c:c + 1],
                                  2.0 ** QKV_EXP, ALU.mult, ALU.mult).then_inc(setup_step, 1)
            dve.tensor_scalar(score_scale[:, :], pair_pow[:, 0:1], -(W_TARGET * 2.0 ** QKV_EXP) ** -2 / 8.0, None,
                              ALU.mult).then_inc(setup_step, 1)
            dve.tensor_scalar(out_scale[:, :], pair_pow[:, 1:2], W_TARGET ** -2 * 2.0 ** -QKV_EXP, None,
                              ALU.mult).then_inc(setup_step, 1)
            for n in range(4):
                dve.wait_ge(w_hi_ready, n + 1)
                dve.scalar_tensor_tensor(out=w_lo[n][:, :, :], in0=w_raw[n][:, :, :], scalar=w_scale[:, n:n + 1],
                                         in1=w_hi[n][:, :, :], op0=ALU.mult, op1=ALU.subtract)\
                    .then_inc(w_lo_ready, 1)
            dve.wait_ge(bias_summed, 1)
            dve.tensor_copy(out_bias[:, :], io_ps[:, 0:hidden]).then_inc(bias_ready, 1)
            dve.wait_ge(setup_step, 13)

            def mask_scores(b):
                s = ring(b.off, 2)
                wait(dve, scores_done, b.count(plus=1))
                wait(dve, mask_ready, b.count(plus=1))
                wait(dve, exp_done, b.count(per=HEADS, plus=-HEADS))
                apart(dve)
                for r in range(2):
                    for j in range(PAIRS):
                        h = r * PAIRS + j
                        dve.tensor_tensor_reduce(neg_scores[:, s, h, :], score_ps[:, r, j * P:(j + 1) * P],
                                                 mask[:, s, :], score_scale[:, :], 3.0e38, ALU.add, ALU.min,
                                                 neg_max[:, s, h:h + 1]).then_inc(masked, 1)

            def ctx_low(b):
                s = ring(b.off, 2)
                wait(dve, ctx_hi_ready, b.count(plus=1))
                dve.scalar_tensor_tensor(out=ctx_lo[:, s, :, :], in0=ctx_ps[:, 0:hidden].rearrange("p (j q) -> p j q", j=KT),
                                         scalar=1.0 / PROB_SCALE, in1=ctx_hi[:, s, :, :], op0=ALU.mult,
                                         op1=ALU.subtract).then_inc(ctx_split, 1)

            def statistics(b):
                s = ring(b.off, 2)
                wait(dve, loaded[ring(b.off, IO)], b.dma_count(IO, 32, 32))
                wait(dve, xn_ready, b.count(plus=-1))
                dve.bn_stats(stats[:, s, :], x_sb[:, ring(b.off, X_RING), :]).then_inc(stats_done, 1)
                wait(dve, stats_done, b.count(per=2, plus=1))
                apart(dve)
                dve.bn_aggr(mean_var[:, s, :], stats[:, s, :]).then_inc(stats_done, 1)

            def qk_high(t):
                g, first = next_pair(t)
                c = t.off % 2
                wait(dve, proj_out, t.batch(2).count(per=KT, plus=KT))
                wait(dve, scores_done, first.count(plus=-2))
                dve.tensor_copy(qk_hi[:, g, c, :, :], qk_full[:, c, :, :]).then_inc(qk_hi_ready, 1)

            def invert(b):
                s = ring(b.off, 2)
                wait(dve, exp_done, b.count(per=HEADS, plus=HEADS))
                wait(dve, normed, b.count(plus=-1))
                dve.reciprocal(inv_sums[:, s, :], sums[:, s, :]).then_inc(inverted, 1)

            def pT_low(b):
                s = ring(b.off, 2)
                wait(dve, pT_hi_ready, b.count(plus=1))
                wait(dve, ctx_done, b.count(plus=-1))
                dve.scalar_tensor_tensor(out=pT_lo[:, s, :, :].rearrange("p (r j) q -> p r (j q)", r=2),
                                         in0=pT_ps[:, :, 0:hidden], scalar=PROB_SCALE,
                                         in1=pT_hi[:, s, :, :].rearrange("p (r j) q -> p r (j q)", r=2),
                                         op0=ALU.mult, op1=ALU.subtract).then_inc(pT_split, 1)

            def finish(b):
                wait(dve, out_done, b.count(plus=1))
                wait(dve, resid_ready, b.count(plus=1))
                wait(dve, stored[ring(b.off, IO)], b.dma_count(IO, 16))
                dve.scalar_tensor_tensor(out=out_sb[:, ring(b.off, IO), :], in0=io_ps[:, 0:hidden],
                                         scalar=out_scale[:, :], in1=x_sb[:, ring(b.off, X_RING), :],
                                         op0=ALU.mult, op1=ALU.add).then_inc(out_ready, 1)

            def v_low(b):
                i = ring(b.off, X_RING)
                wait(dve, v_hi_ready, b.count(plus=1))
                dve.scalar_tensor_tensor(out=v_lo[:, i, :], in0=proj_ps[1][:, 0:hidden], scalar=PROJ_SCALE,
                                         in1=v_hi[:, i, :], op0=ALU.mult, op1=ALU.subtract).then_inc(v_split, 1)

            def hT_low(b):
                g, cols = pair_of(b)
                wait(dve, hT_hi_ready, b.count(plus=1))
                dve.scalar_tensor_tensor(out=hT_lo[:, g, :, cols], in0=io_ps[:, 0:hidden].rearrange("p (j q) -> p j q", j=KT),
                                         scalar=0.0, in1=hT_hi[:, g, :, cols], op0=ALU.max,
                                         op1=ALU.subtract).then_inc(hT_split, 1)

            def slot(t):
                b = t.batch(0)
                if b.exists(batches):
                    mask_scores(b)
                b = t.batch(-2)
                if b.exists(batches):
                    ctx_low(b)
                b = t.batch(5)
                if b.exists(batches):
                    statistics(b)
                if t.batch(2).exists(batches):
                    qk_high(t)
                b = t.batch(0)
                if b.exists(batches):
                    invert(b)
                b = t.batch(-1)
                if b.exists(batches):
                    pT_low(b)
                b = t.batch(-2)
                if b.exists(batches):
                    finish(b)
                b = t.batch(2)
                if b.exists(batches):
                    v_low(b)
                b = t.batch(4)
                if b.exists(batches):
                    hT_low(b)

            slots(dve, batches, slot)

        @block.tensor
        def _(pe):
            def product(dst, lhs, rhs, tiles, start=True):
                passes = [(0, 1), (1, 0), (0, 0)]
                n, total = 0, len(tiles) * len(passes)
                for k in tiles:
                    for a, b in passes:
                        last = pe.matmul(dst, lhs[a](k), rhs[b](k), start=(n == 0), stop=(n == total - 1))
                        n += 1
                return last

            pe.wait_ge(bias_ready, 1)
            pe.wait_ge(consts_loaded, 64)
            pe.wait_ge(w_loaded[3], 16)
            pe.wait_ge(ident_ready, 4)
            for j in range(KT):
                pe.matmul(io_ps[:, 0:hidden], bv_rep[:, j, :], w_raw[3][:, j, :], start=(j == 0), stop=False)
            pe.matmul(io_ps[:, 0:hidden], ones_row[:, :], bf_row[:, :], start=False, stop=True)\
                .then_inc(bias_summed, 1)
            pe.wait_ge(bias_ready, 2)

            def scores(b):
                g, cols = pair_of(b)
                wait(pe, qk_split, Batch(b.base, b.off // 2 * 2).count(plus=2))
                wait(pe, masked, b.count(per=HEADS))
                q, k = (qk_hi[:, g, 0, :, cols], qk_lo[:, g, 0, :, cols]), (qk_hi[:, g, 1, :, cols], qk_lo[:, g, 1, :, cols])
                for j in range(PAIRS):
                    for n, (a, c) in enumerate([(0, 1), (1, 0), (0, 0)]):
                        for r in range(2):
                            rows = slice(r * DH, (r + 1) * DH)
                            last = pe.matmul(score_ps[:, r, j * P:(j + 1) * P], q[a][rows, j, :], k[c][rows, j, :],
                                             start=(n == 0), stop=(n == 2))
                last.then_inc(scores_done, 1)

            def project(t, j):
                g, first = next_pair(t)
                c = t.off % 2
                if j == 0:
                    wait(pe, hT_split, first.count(plus=2))
                    wait(pe, proj_out, t.batch(2).count(per=KT))
                    if isinstance(t.base, int):
                        wait(pe, w_lo_ready, c + 1)
                elif j == 1:
                    wait(pe, v_split, t.batch(2).count())
                else:
                    wait(pe, proj_out, t.batch(2).count(per=KT, plus=1))
                product(proj_ps[j % 2][:, 0:2 * P],
                        [lambda k, w=w: w[c][:, k, j * P:(j + 1) * P] for w in (w_hi, w_lo)],
                        [lambda k, h=h: h[:, g, k, :] for h in (hT_hi, hT_lo)], range(KT)).then_inc(proj_done, 1)

            def project_v(b):
                g, cols = pair_of(b)
                if isinstance(b.base, int):
                    wait(pe, w_lo_ready, 3)
                wait(pe, proj_out, b.count(per=KT, plus=2))
                product(proj_ps[1][:, 0:hidden],
                        [lambda k, h=h: h[:, g, k, cols] for h in (hT_hi, hT_lo)],
                        [lambda k, w=w: w[2][:, k, :] for w in (w_hi, w_lo)], range(KT)).then_inc(v_done, 1)

            def transpose_h(b):
                wait(pe, xn_ready, b.count(plus=1))
                wait(pe, hT_split, b.count())
                wait(pe, out_ready, b.count(plus=-5))
                for j in range(KT):
                    last = pe.transpose(io_ps[:, j * P:(j + 1) * P], xn[:, ring(b.off, XN), j * P:(j + 1) * P], ident[:, :])
                last.then_inc(hT_done, 1)

            def transpose_probs(b):
                wait(pe, normed, b.count(plus=1))
                wait(pe, pT_split, b.count())
                for h in range(HEADS):
                    r, j = h // PAIRS, h % PAIRS
                    last = pe.transpose(pT_ps[:, r, j * P:(j + 1) * P], probs_n[:, ring(b.off, 2), h, :], ident[:, :])
                last.then_inc(pT_done, 1)

            def attend(b):
                s, i = ring(b.off, 2), ring(b.off, X_RING)
                wait(pe, pT_split, b.count(plus=1))
                wait(pe, v_split, b.count(plus=1))
                wait(pe, ctx_split, b.count())
                v, p = (v_hi, v_lo), (pT_hi, pT_lo)
                for j in range(PAIRS):
                    for n, (a, c) in enumerate([(0, 1), (1, 0), (0, 0)]):
                        for r in range(2):
                            head = 2 * j + r
                            last = pe.matmul(ctx_ps[r * DH:(r + 1) * DH, j * P:(j + 1) * P],
                                             v[a][:, i, head * DH:(head + 1) * DH], p[c][:, s, r * PAIRS + j, :],
                                             start=(n == 0), stop=(n == 2))
                last.then_inc(ctx_done, 1)

            def project_out(b):
                s = ring(b.off, 2)
                wait(pe, ctx_split, b.count(plus=1))
                split = b.count(plus=6)
                wait(pe, hT_split, min(split, batches) if isinstance(split, int) else split)
                if isinstance(b.base, int):
                    wait(pe, w_lo_ready, 4)
                product(io_ps[:, 0:hidden], [lambda k, c=c: c[:, s, k, :] for c in (ctx_hi, ctx_lo)],
                        [lambda k, w=w: w[3][:, k, :] for w in (w_hi, w_lo)], range(KT)).then_inc(out_done, 1)

            def slot(t):
                b = t.batch(0)
                if b.exists(batches):
                    scores(b)
                projecting = t.batch(2).exists(batches)
                if projecting:
                    project(t, 0)
                b = t.batch(-2)
                if b.exists(batches):
                    attend(b)
                if projecting:
                    project(t, 1)
                    project(t, 2)
                b = t.batch(-1)
                if b.exists(batches):
                    transpose_probs(b)
                b = t.batch(-2)
                if b.exists(batches):
                    project_out(b)
                b = t.batch(2)
                if b.exists(batches):
                    project_v(b)
                b = t.batch(4)
                if b.exists(batches):
                    transpose_h(b)

            slots(pe, batches, slot)


_INS = ["x", "adj", "L0_gnn_Wq", "L0_gnn_bq", "L0_gnn_Wk", "L0_gnn_bk", "L0_gnn_Wv", "L0_gnn_bv", "L0_gnn_Wf", "L0_gnn_bf"]


def kernel(**inputs):
    import numpy as _np
    import concourse.bacc as _bacc
    from concourse import mybir as _mybir
    from concourse.bass_utils import run_bass_kernel_spmd as _run

    nc = _bacc.Bacc("TRN2", target_bir_lowering=False, num_devices=1)
    arrays, args = {}, []
    for name in _INS:
        a = _np.ascontiguousarray(inputs[name])
        arrays[f"in_{name}_dram"] = a
        args.append(nc.dram_tensor(f"in_{name}_dram", a.shape, _mybir.dt.from_np(a.dtype), kind="ExternalInput").ap())
    x = arrays["in_x_dram"]
    out = nc.dram_tensor("out_dram", x.shape, _mybir.dt.float32, kind="ExternalOutput").ap()
    graph_attention(nc, *args, out)
    r = _run(nc, [arrays], core_ids=[0])
    return r.results[0]["out_dram"]
```

```python
import concourse.bass as bass
from concourse import mybir

F32 = mybir.dt.float32
F16 = mybir.dt.float16
U8 = mybir.dt.uint8
U32 = mybir.dt.uint32
ALU = mybir.AluOpType
ACT = mybir.ActivationFunctionType
AX = mybir.AxisListType

P = 128
HEADS = 6
DH = 64
EPS = 1e-5
NEG = -9000000000000000.0

H_SCALE = 2.0 ** 11
PROJ_SCALE = 2.0 ** -19
QKV_EXP = -8
PROB_SCALE = 2.0 ** 15
W_TARGET = 2.0 ** 13
W_FLOOR = 2.0 ** -26

UNROLL = 8
LAST_LAG = 3
LEAD = 6


def ring(b, n):
    return b % n


class Step:

    def __init__(self, base, off):
        self.base, self.off = base, off

    def base_or_none(self):
        return self.base if isinstance(self.base, int) else None

    def batch(self, lag):
        return Batch(self.base, self.off + lag)


class Batch:
    def __init__(self, base, off):
        self.base, self.off = base, off

    def exists(self, batches):
        return not isinstance(self.base, int) or 0 <= self.base + self.off < batches

    def count(self, per=1, plus=0):
        return self.base * per + (self.off * per + plus)

    def dma_count(self, n, per, plus=0):
        if isinstance(self.base, int):
            return (self.base + self.off) // n * per + plus
        return self.base * (per // n) + (self.off // n * per + plus)


def wait(eng, sem, value):
    if not isinstance(value, int) or value > 0:
        eng.wait_ge(sem, value)


def apart(eng):
    eng.nop(nofuse=True)


def slots(eng, batches, body, setup={}):
    for t in range(-LEAD, UNROLL):
        if t in setup:
            setup[t]()
        body(Step(0, t))
    with eng.Fori(1, batches // UNROLL - 1) as n:
        for off in range(UNROLL):
            body(Step(n * UNROLL, off))
    for off in range(UNROLL + LAST_LAG):
        body(Step(batches - UNROLL, off))


def graph_attention(nc, x, adj, Wq, bq, Wk, bk, Wv, bv, Wf, bf, out):
    batches, tokens, hidden = x.shape
    assert tokens == P and hidden == HEADS * DH and batches % UNROLL == 0
    KT = hidden // P
    PAIRS = HEADS // 2
    assert PAIRS == KT

    from contextlib import ExitStack
    with ExitStack() as ctx:
        def sb(name, shape, dt=F32):
            return ctx.enter_context(nc.sbuf_tensor(name, shape, dt))

        def bank(name):
            return ctx.enter_context(nc.psum_tensor(name, [P, 512], F32))

        def sem(name):
            return ctx.enter_context(nc.semaphore(name))

        ones_row = sb("ones_row", [1, P])
        w_raw = [sb(f"w_raw_{n}", [P, KT, hidden]) for n in "qkvf"]
        w_hi = [sb(f"w_hi_{n}", [P, KT, hidden], F16) for n in "qkvf"]
        w_lo = [sb(f"w_lo_{n}", [P, KT, hidden], F16) for n in "qkvf"]
        extremes = sb("extremes", [P, 10])
        ext_all = sb("ext_all", [P, 10])
        bias_max = sb("bias_max", [P, 2])
        top = sb("top", [P, 4])
        top_pow = sb("top_pow", [P, 4])
        top_rec = sb("top_rec", [P, 4])
        w_scale = sb("w_scale", [P, 4])
        pair_pow = sb("pair_pow", [P, 2])
        pair_scale = sb("pair_scale", [P, 1])
        score_scale = sb("score_scale", [P, 1])
        out_scale = sb("out_scale", [P, 1])
        mask_scale = sb("mask_scale", [P, 2])
        qk_bias = sb("qk_bias", [P, 2, KT])
        bv_col = sb("bv_col", [P, KT])
        bv_rep = sb("bv_rep", [P, KT, P])
        bf_row = sb("bf_row", [1, hidden])
        out_bias = sb("out_bias", [P, hidden])

        X_RING, XN, IO = 8, 2, 4
        x_sb = sb("x_sb", [P, X_RING, hidden])
        adj_sb = sb("adj_sb", [P, X_RING, P], U8)
        stats = sb("stats", [P, 2, 6])
        mean_var = sb("mean_var", [P, 2, 2])
        var_eps = sb("var_eps", [P, 2, 1])
        neg_mean = sb("neg_mean", [P, 2, 1])
        rstd = sb("rstd", [P, 2, 1])
        half_power = sb("half_power", [P, 1])
        resid = sb("resid", [P, X_RING, hidden])
        xn = sb("xn", [P, XN, hidden])
        h_parts = sb("h_parts", [P, 2, 2, hidden], F16)
        hT = sb("hT", [P, 2, 2, KT, 2 * P], F16)
        qk_full = sb("qk_full", [P, 2, KT, 2 * P])
        qk_hi = sb("qk_hi", [P, 2, 2, KT, 2 * P], F16)
        qk_lo = sb("qk_lo", [P, 2, 2, KT, 2 * P], F16)
        v_hi = sb("v_hi", [P, X_RING, hidden], F16)
        v_lo = sb("v_lo", [P, X_RING, hidden], F16)
        mask = sb("mask", [P, 2, P])
        neg_scores = sb("neg_scores", [P, 2, HEADS, P])
        neg_max = sb("neg_max", [P, 2, HEADS])
        probs = sb("probs", [P, 2, HEADS, P])
        sums = sb("sums", [P, 2, HEADS])
        inv_sums = sb("inv_sums", [P, 2, HEADS])
        probs_n = sb("probs_n", [P, 2, HEADS, P])
        p_parts = sb("p_parts", [P, 2, 2, HEADS, P], F16)
        pT = sb("pT", [P, 2, 2, HEADS, P], F16)
        ctx_hi = sb("ctx_hi", [P, 2, KT, P], F16)
        ctx_lo = sb("ctx_lo", [P, 2, KT, P], F16)
        out_sb = sb("out_sb", [P, IO, hidden])

        score_ps = ctx.enter_context(nc.psum_tensor("score_ps", [P, 2, 512], F32))
        ctx_ps = [bank("ctx_ps0"), bank("ctx_ps1")]
        out_ps = [bank("out_ps0"), bank("out_ps1")]
        proj_ps = [bank("proj_ps0"), bank("proj_ps1")]

        consts_loaded = sem("consts_loaded")
        w_loaded = [sem(f"w_loaded_{n}") for n in "qkvf"]
        loaded = [sem(f"loaded{i}") for i in range(IO)]
        stored = [sem(f"stored{i}") for i in range(IO)]
        fills_ready = sem("fills_ready")
        ext_ready = sem("ext_ready")
        ext_reduced = sem("ext_reduced")
        setup_step = sem("setup_step")
        w_hi_ready = sem("w_hi_ready")
        w_lo_ready = sem("w_lo_ready")
        bias_summed = sem("bias_summed")
        bias_ready = sem("bias_ready")
        stats_done = sem("stats_done")
        ln_step = sem("ln_step")
        xn_ready = sem("xn_ready")
        resid_ready = sem("resid_ready")
        h_hi_ready = sem("h_hi_ready")
        h_split = sem("h_split")
        h_turned = [sem(f"h_turned{i}") for i in range(4)]
        proj_done = sem("proj_done")
        proj_out = sem("proj_out")
        qk_hi_ready = sem("qk_hi_ready")
        qk_split = sem("qk_split")
        v_done = sem("v_done")
        v_hi_ready = sem("v_hi_ready")
        v_split = sem("v_split")
        mask_ready = sem("mask_ready")
        scores_done = sem("scores_done")
        masked = sem("masked")
        exp_done = sem("exp_done")
        inverted = sem("inverted")
        normed = sem("normed")
        p_hi_ready = sem("p_hi_ready")
        p_split = sem("p_split")
        p_turned = [sem(f"p_turned{i}") for i in range(2)]
        ctx_done = sem("ctx_done")
        ctx_hi_ready = sem("ctx_hi_ready")
        ctx_split = sem("ctx_split")
        out_done = sem("out_done")
        out_ready = sem("out_ready")

        W_ORDER = (0, 2, 1, 3)
        W_PLACE = {n: i for i, n in enumerate(W_ORDER)}

        block = ctx.enter_context(nc.Block())

        def pair_of(b):
            o = b.off
            return o // 2 % 2, slice(o % 2 * P, (o % 2 + 1) * P)

        def next_pair(t):
            b = Batch(t.base, t.off // 2 * 2 + 2)
            return b.off // 2 % 2, b

        @block.sync
        def _(sp):
            def load(b):
                i = ring(b.off, X_RING)
                wait(sp, resid_ready, b.count(plus=1 - X_RING))
                apart(sp)
                wait(sp, mask_ready, b.count(plus=1 - X_RING))
                apart(sp)
                wait(sp, xn_ready, b.count(plus=1 - IO))
                apart(sp)
                got = loaded[ring(b.off, IO)]
                if isinstance(b.base, int):
                    src_x, src_adj = x[b.base + b.off], adj[b.base + b.off]
                else:
                    n = b.base + b.off
                    src_x = x[bass.ds(n, 1)].rearrange("o p h -> (o p) h")
                    src_adj = adj[bass.ds(n, 1)].rearrange("o p h -> (o p) h")
                sp.dma_start(x_sb[:, i, :], src_x).then_inc(got, 16)
                sp.dma_start(adj_sb[:, i, :], src_adj).then_inc(got, 16)

            def store(b):
                wait(sp, out_ready, b.count(plus=1))
                apart(sp)
                if isinstance(b.base, int):
                    dst = out[b.base + b.off]
                else:
                    dst = out[bass.ds(b.base + b.off, 1)].rearrange("o p h -> (o p) h")
                sp.dma_start(dst, out_sb[:, ring(b.off, IO), :]).then_inc(stored[ring(b.off, IO)], 16)

            load(Batch(0, 0))
            load(Batch(0, 1))
            sp.dma_start(extremes[:, 4:7], bq.rearrange("(t p) -> p t", p=P), allow_slow_non_contiguous=True).then_inc(consts_loaded, 16)
            sp.dma_start(extremes[:, 7:10], bk.rearrange("(t p) -> p t", p=P), allow_slow_non_contiguous=True).then_inc(consts_loaded, 16)
            sp.dma_start(bv_col[:, :], bv.rearrange("(t p) -> p t", p=P), allow_slow_non_contiguous=True).then_inc(consts_loaded, 16)
            sp.dma_start(bf_row[:, :], bf.rearrange("(o n) -> o n", o=1)).then_inc(consts_loaded, 16)
            sp.dma_start(w_raw[0][:, :, :], Wq.rearrange("(t p) n -> p t n", p=P)).then_inc(w_loaded[0], 16)
            sp.dma_start(w_raw[1][:, :, :], Wk.rearrange("(t p) n -> p t n", p=P)).then_inc(w_loaded[1], 16)
            sp.dma_start(w_raw[2][:, :, :], Wv.rearrange("(t p) n -> p t n", p=P)).then_inc(w_loaded[2], 16)
            load(Batch(0, 2))
            sp.dma_start(w_raw[3][:, :, :], Wf.rearrange("(t p) n -> p t n", p=P)).then_inc(w_loaded[3], 16)

            def turn_h(b):
                g, cols = pair_of(b)
                wait(sp, h_split, b.count(plus=1))
                apart(sp)
                wait(sp, v_done, Batch(b.base, b.off // 2 * 2).count(plus=-2))
                apart(sp)
                sp.dma_start_transpose(hT[:, g, :, :, cols].rearrange("p c j q -> p (c j) q"),
                                       h_parts[:, ring(b.off, 2), :, :].rearrange("p c n -> p (c n)"))\
                    .then_inc(h_turned[ring(b.off, 4)], 16)

            def turn_p(b):
                s = ring(b.off, 2)
                wait(sp, p_split, b.count(plus=1))
                apart(sp)
                wait(sp, ctx_done, b.count(plus=-1))
                apart(sp)
                sp.dma_start_transpose(pT[:, s, :, :, :].rearrange("p c h q -> p (c h) q"),
                                       p_parts[:, s, :, :, :].rearrange("p c h k -> p (c h k)"))\
                    .then_inc(p_turned[s], 16)

            def slot(t):
                b = t.batch(6)
                if b.exists(batches) and not (isinstance(t.base, int) and 0 <= t.base + b.off < 3):
                    load(b)
                b = t.batch(4)
                if b.exists(batches):
                    turn_h(b)
                b = t.batch(-3)
                if b.exists(batches):
                    store(b)
                b = t.batch(-1)
                if b.exists(batches):
                    turn_p(b)

            slots(sp, batches, slot)
            for i in range(IO):
                sp.wait_ge(stored[i], 16 * (batches // IO))

        @block.gpsimd
        def _(pool):
            pool.memset(ones_row[:, :], 1.0).then_inc(fills_ready, 1)
            pool.memset(half_power[:, :], -0.5).then_inc(fills_ready, 1)
            pool.wait_ge(fills_ready, 2)

            def reduce_extremes():
                pool.wait_ge(ext_ready, 4)
                pool.wait_ge(consts_loaded, 64)
                pool.partition_all_reduce(ext_all[:, :], extremes[:, :], P, bass.bass_isa.ReduceOp.absmax)\
                    .then_inc(ext_reduced, 1)

            def make_mask(b):
                wait(pool, masked, b.count(per=HEADS, plus=-HEADS))
                if isinstance(b.base, int) and b.base + b.off == 0:
                    pool.wait_ge(setup_step, 9)
                apart(pool)
                pool.tensor_scalar(mask[:, ring(b.off, 2), :], adj_sb[:, ring(b.off, X_RING), :],
                                   mask_scale[:, 0:1], mask_scale[:, 1:2], ALU.mult, ALU.add)\
                    .then_inc(mask_ready, 1)

            def layer_norm(b):
                s = ring(b.off, 2)
                xb = x_sb[:, ring(b.off, X_RING), :]
                wait(pool, loaded[ring(b.off, IO)], b.dma_count(IO, 32, 32))
                wait(pool, stats_done, b.count(per=2, plus=2))
                apart(pool)
                pool.tensor_scalar(var_eps[:, s, :], mean_var[:, s, 1:2], EPS, H_SCALE ** -2, ALU.add, ALU.mult)\
                    .then_inc(ln_step, 1)
                pool.tensor_scalar(neg_mean[:, s, :], mean_var[:, s, 0:1], -1.0, 0.0, ALU.mult, ALU.add)\
                    .then_inc(ln_step, 1)
                wait(pool, ln_step, b.count(per=3, plus=2))
                pool.tensor_tensor(rstd[:, s, :], var_eps[:, s, :], half_power[:, :], ALU.pow).then_inc(ln_step, 1)
                wait(pool, ln_step, b.count(per=3, plus=3))
                wait(pool, h_split, b.count(plus=-1))
                apart(pool)
                pool.tensor_scalar(xn[:, ring(b.off, XN), :], xb, neg_mean[:, s, :], rstd[:, s, :],
                                   ALU.add, ALU.mult).then_inc(xn_ready, 1)

            def residual(b):
                i = ring(b.off, X_RING)
                if isinstance(b.base, int) and b.base + b.off == 0:
                    pool.wait_ge(bias_ready, 2)
                wait(pool, out_ready, b.count(plus=1 - X_RING))
                pool.tensor_tensor(resid[:, i, :], x_sb[:, i, :], out_bias[:, :], ALU.add).then_inc(resid_ready, 1)

            def qk_low(t):
                g, first = next_pair(t)
                c = t.off % 2
                wait(pool, qk_hi_ready, t.batch(2).count(plus=1))
                wait(pool, scores_done, first.count(plus=-2))
                pool.tensor_tensor(qk_lo[:, g, c, :, :], qk_full[:, c, :, :], qk_hi[:, g, c, :, :], ALU.subtract)\
                    .then_inc(qk_split, 1)

            def normalise(b):
                s = ring(b.off, 2)
                wait(pool, exp_done, b.count(per=HEADS, plus=HEADS))
                wait(pool, inverted, b.count(plus=1))
                wait(pool, p_split, b.count(plus=-1))
                pool.tensor_tensor(probs_n[:, s, :, :], probs[:, s, :, :],
                                   inv_sums[:, s, :].unsqueeze(2).to_broadcast([P, HEADS, P]), ALU.mult)\
                    .then_inc(normed, 1)

            def slot(t):
                b = t.batch(-1)
                if b.exists(batches):
                    normalise(b)
                b = t.batch(5)
                if b.exists(batches):
                    layer_norm(b)
                b = t.batch(1)
                if b.exists(batches):
                    make_mask(b)
                if t.batch(2).exists(batches):
                    if t.base_or_none() == 0 and t.off < 0:
                        qk_low(t)
                        residual(t.batch(2))
                    else:
                        residual(t.batch(2))
                        qk_low(t)

            slots(pool, batches, slot, {-2: reduce_extremes})

        @block.scalar
        def _(act):
            def weights_high():
                act.wait_ge(setup_step, 5)
                for n in W_ORDER:
                    act.wait_ge(w_loaded[n], 16)
                    act.activation(w_hi[n][:, :, :], w_raw[n][:, :, :], ACT.Copy, scale=w_scale[:, n:n + 1])\
                        .then_inc(w_hi_ready, 1)

            def qk_out(t, j):
                c = t.off % 2
                b = t.batch(2)
                wait(act, proj_done, b.count(per=KT, plus=j + 1))
                if j == 0:
                    wait(act, qk_split, b.count(plus=-1))
                    if isinstance(t.base, int) and b.base + b.off == 0:
                        act.wait_ge(setup_step, 11)
                act.activation(qk_full[:, c, j, :], proj_ps[j % 2][:, 0:2 * P], ACT.Identity,
                               bias=qk_bias[:, c, j:j + 1], scale=PROJ_SCALE).then_inc(proj_out, 1)

            def exps(b, heads):
                s = ring(b.off, 2)
                for h in heads:
                    if h == 0:
                        wait(act, normed, b.count(plus=-1))
                    wait(act, masked, b.count(per=HEADS, plus=h + 1))
                    act.activation(probs[:, s, h, :], neg_scores[:, s, h, :], ACT.Exp, scale=-1.0,
                                   bias=neg_max[:, s, h:h + 1], accum_out=sums[:, s, h:h + 1])\
                        .then_inc(exp_done, 1)

            def ctx_high(b):
                wait(act, ctx_done, b.count(plus=1))
                wait(act, out_done, b.count(plus=-1))
                act.activation(ctx_hi[:, ring(b.off, 2), :, :], ctx_ps[ring(b.off, 2)][:, 0:hidden].rearrange("p (j q) -> p j q", j=KT),
                               ACT.Copy, scale=1.0 / PROB_SCALE).then_inc(ctx_hi_ready, 1)

            def p_high(b):
                s = ring(b.off, 2)
                wait(act, normed, b.count(plus=1))
                wait(act, p_turned[s], b.dma_count(2, 16))
                act.activation(p_parts[:, s, 0, :, :], probs_n[:, s, :, :], ACT.Copy, scale=PROB_SCALE)\
                    .then_inc(p_hi_ready, 1)

            def v_high(b):
                wait(act, v_done, b.count(plus=1))
                wait(act, ctx_done, b.count(plus=1 - X_RING))
                act.activation(v_hi[:, ring(b.off, X_RING), :], proj_ps[1][:, 0:hidden], ACT.Copy,
                               scale=PROJ_SCALE).then_inc(v_hi_ready, 1)

            def h_high(b):
                s = ring(b.off, 2)
                wait(act, xn_ready, b.count(plus=1))
                two_back = Batch(b.base, b.off - 2)
                if two_back.exists(batches):
                    wait(act, h_turned[ring(two_back.off, 4)], two_back.dma_count(4, 16, 16))
                act.activation(h_parts[:, s, 0, :], xn[:, s, :], ACT.Relu).then_inc(h_hi_ready, 1)

            def slot(t):
                scored, used, turned, coming = t.batch(0), t.batch(-2), t.batch(-1), t.batch(5)
                projecting = t.batch(2).exists(batches)
                if projecting:
                    qk_out(t, 0)
                if turned.exists(batches):
                    p_high(turned)
                if scored.exists(batches):
                    exps(scored, range(0, PAIRS))
                if used.exists(batches):
                    ctx_high(used)
                if projecting:
                    qk_out(t, 1)
                    qk_out(t, 2)
                if scored.exists(batches):
                    exps(scored, range(PAIRS, HEADS))
                if coming.exists(batches):
                    h_high(coming)
                if projecting:
                    v_high(t.batch(2))

            slots(act, batches, slot, {-2: weights_high})

        @block.vector
        def _(dve):
            def maxima(ns):
                for n in ns:
                    dve.wait_ge(w_loaded[n], 16)
                    dve.tensor_reduce(extremes[:, n:n + 1], w_raw[n][:, :, :], AX.XY, ALU.max,
                                      apply_absolute_value=True).then_inc(ext_ready, 1)

            def setup_maxima():
                statistics(Batch(0, 1))
                maxima((0,))

            def setup_scales():
                maxima((3,))
                dve.wait_ge(consts_loaded, 64)
                for j in range(KT):
                    last = dve.tensor_copy(bv_rep[:, j, :], bv_col[:, j:j + 1].to_broadcast([P, P]))
                last.then_inc(bias_ready, 1)
                dve.wait_ge(ext_reduced, 1)
                dve.tensor_reduce(bias_max[:, :], ext_all[:, 4:10].rearrange("p (c t) -> p c t", c=2), AX.X, ALU.max)\
                    .then_inc(setup_step, 1)
                dve.tensor_scalar(top[:, 2:4], ext_all[:, 2:4], W_FLOOR, None, ALU.max).then_inc(setup_step, 1)
                dve.wait_ge(setup_step, 2)
                dve.scalar_tensor_tensor(out=top[:, 0:2], in0=bias_max[:, :], scalar=2.0 ** QKV_EXP, in1=ext_all[:, 0:2],
                                         op0=ALU.mult, op1=ALU.max).then_inc(setup_step, 1)
                dve.wait_ge(setup_step, 3)
                dve.tensor_scalar(top_rec[:, :], top[:, :], W_FLOOR, None, ALU.max).then_inc(ext_ready, 1)
                dve.wait_ge(ext_ready, 5)
                dve.tensor_scalar(top_pow[:, :].bitcast(U32), top_rec[:, :].bitcast(U32), 0x7f800000, None,
                                  ALU.bitwise_and).then_inc(ext_ready, 1)
                dve.wait_ge(ext_ready, 6)
                dve.reciprocal(top_rec[:, :], top_pow[:, :]).then_inc(setup_step, 1)
                dve.wait_ge(setup_step, 4)
                dve.tensor_scalar(w_scale[:, :], top_rec[:, :], W_TARGET, None, ALU.mult).then_inc(setup_step, 1)
                dve.wait_ge(setup_step, 5)
                pows = top_pow[:, :].rearrange("p (c t) -> p c t", t=2)
                dve.tensor_tensor(pair_pow[:, :], pows[:, :, 0], pows[:, :, 1], ALU.mult).then_inc(setup_step, 1)
                dve.tensor_tensor(pair_scale[:, :], w_scale[:, 0:1], w_scale[:, 1:2], ALU.mult).then_inc(setup_step, 1)
                dve.wait_ge(setup_step, 7)
                dve.tensor_scalar(mask_scale[:, 0:1], pair_scale[:, :], -NEG * 8.0 * 2.0 ** (2 * QKV_EXP), None, ALU.mult)\
                    .then_inc(setup_step, 1)
                dve.tensor_scalar(mask_scale[:, 1:2], pair_scale[:, :], NEG * 8.0 * 2.0 ** (2 * QKV_EXP), None, ALU.mult)\
                    .then_inc(setup_step, 1)
                for c in range(2):
                    dve.tensor_scalar(qk_bias[:, c, :], extremes[:, 4 + KT * c:4 + KT * (c + 1)], w_scale[:, c:c + 1],
                                      2.0 ** QKV_EXP, ALU.mult, ALU.mult).then_inc(setup_step, 1)
                dve.tensor_scalar(score_scale[:, :], pair_pow[:, 0:1], -(W_TARGET * 2.0 ** QKV_EXP) ** -2 / 8.0, None,
                                  ALU.mult).then_inc(setup_step, 1)
                dve.tensor_scalar(out_scale[:, :], pair_pow[:, 1:2], W_TARGET ** -2 * 2.0 ** -QKV_EXP, None,
                                  ALU.mult).then_inc(setup_step, 1)

            def weights_low():
                for i, n in enumerate(W_ORDER):
                    dve.wait_ge(w_hi_ready, i + 1)
                    dve.scalar_tensor_tensor(out=w_lo[n][:, :, :], in0=w_raw[n][:, :, :], scalar=w_scale[:, n:n + 1],
                                             in1=w_hi[n][:, :, :], op0=ALU.mult, op1=ALU.subtract)\
                        .then_inc(w_lo_ready, 1)
                dve.wait_ge(bias_summed, 1)
                dve.tensor_copy(out_bias[:, :], ctx_ps[0][:, 0:hidden]).then_inc(bias_ready, 1)
                dve.wait_ge(setup_step, 13)

            def mask_scores(b):
                s = ring(b.off, 2)
                wait(dve, scores_done, b.count(plus=1))
                wait(dve, mask_ready, b.count(plus=1))
                wait(dve, exp_done, b.count(per=HEADS, plus=-HEADS))
                apart(dve)
                for r in range(2):
                    for j in range(PAIRS):
                        h = r * PAIRS + j
                        dve.tensor_tensor_reduce(neg_scores[:, s, h, :], score_ps[:, r, j * P:(j + 1) * P],
                                                 mask[:, s, :], score_scale[:, :], 3.0e38, ALU.add, ALU.min,
                                                 neg_max[:, s, h:h + 1]).then_inc(masked, 1)

            def ctx_low(b):
                s = ring(b.off, 2)
                wait(dve, ctx_hi_ready, b.count(plus=1))
                dve.scalar_tensor_tensor(out=ctx_lo[:, s, :, :], in0=ctx_ps[ring(b.off, 2)][:, 0:hidden].rearrange("p (j q) -> p j q", j=KT),
                                         scalar=1.0 / PROB_SCALE, in1=ctx_hi[:, s, :, :], op0=ALU.mult,
                                         op1=ALU.subtract).then_inc(ctx_split, 1)

            def statistics(b):
                s = ring(b.off, 2)
                wait(dve, loaded[ring(b.off, IO)], b.dma_count(IO, 32, 32))
                wait(dve, xn_ready, b.count(plus=-1))
                dve.bn_stats(stats[:, s, :], x_sb[:, ring(b.off, X_RING), :]).then_inc(stats_done, 1)
                wait(dve, stats_done, b.count(per=2, plus=1))
                apart(dve)
                dve.bn_aggr(mean_var[:, s, :], stats[:, s, :]).then_inc(stats_done, 1)

            def qk_high(t):
                g, first = next_pair(t)
                c = t.off % 2
                wait(dve, proj_out, t.batch(2).count(per=KT, plus=KT))
                wait(dve, scores_done, first.count(plus=-2))
                dve.tensor_copy(qk_hi[:, g, c, :, :], qk_full[:, c, :, :]).then_inc(qk_hi_ready, 1)

            def invert(b):
                s = ring(b.off, 2)
                wait(dve, exp_done, b.count(per=HEADS, plus=HEADS))
                wait(dve, normed, b.count(plus=-1))
                dve.reciprocal(inv_sums[:, s, :], sums[:, s, :]).then_inc(inverted, 1)

            def p_low(b):
                s = ring(b.off, 2)
                wait(dve, p_hi_ready, b.count(plus=1))
                dve.scalar_tensor_tensor(out=p_parts[:, s, 1, :, :], in0=probs_n[:, s, :, :], scalar=PROB_SCALE,
                                         in1=p_parts[:, s, 0, :, :], op0=ALU.mult, op1=ALU.subtract)\
                    .then_inc(p_split, 1)

            def finish(b):
                wait(dve, out_done, b.count(plus=1))
                wait(dve, resid_ready, b.count(plus=1))
                wait(dve, stored[ring(b.off, IO)], b.dma_count(IO, 16))
                dve.scalar_tensor_tensor(out=out_sb[:, ring(b.off, IO), :], in0=out_ps[ring(b.off, 2)][:, 0:hidden],
                                         scalar=out_scale[:, :], in1=resid[:, ring(b.off, X_RING), :],
                                         op0=ALU.mult, op1=ALU.add).then_inc(out_ready, 1)

            def v_low(b):
                i = ring(b.off, X_RING)
                wait(dve, v_hi_ready, b.count(plus=1))
                dve.scalar_tensor_tensor(out=v_lo[:, i, :], in0=proj_ps[1][:, 0:hidden], scalar=PROJ_SCALE,
                                         in1=v_hi[:, i, :], op0=ALU.mult, op1=ALU.subtract).then_inc(v_split, 1)

            def h_low(b):
                s = ring(b.off, 2)
                wait(dve, h_hi_ready, b.count(plus=1))
                dve.scalar_tensor_tensor(out=h_parts[:, s, 1, :], in0=xn[:, s, :], scalar=0.0,
                                         in1=h_parts[:, s, 0, :], op0=ALU.max, op1=ALU.subtract)\
                    .then_inc(h_split, 1)

            def slot(t):
                b = t.batch(5)
                if b.exists(batches) and not (isinstance(t.base, int) and t.base + b.off == 1):
                    statistics(b)
                b = t.batch(0)
                if b.exists(batches):
                    mask_scores(b)
                b = t.batch(-1)
                if b.exists(batches):
                    p_low(b)
                b = t.batch(-2)
                if b.exists(batches):
                    ctx_low(b)
                if t.batch(2).exists(batches):
                    qk_high(t)
                b = t.batch(0)
                if b.exists(batches):
                    invert(b)
                b = t.batch(2)
                if b.exists(batches):
                    v_low(b)
                b = t.batch(-2)
                if b.exists(batches):
                    finish(b)
                b = t.batch(5)
                if b.exists(batches):
                    h_low(b)

            slots(dve, batches, slot,
                  {-4: setup_maxima, -3: lambda: maxima((1, 2)), -2: lambda: (setup_scales(), weights_low())})

        @block.tensor
        def _(pe):
            def product(dst, lhs, rhs, tiles, start=True):
                passes = [(0, 1), (1, 0), (0, 0)]
                n, total = 0, len(tiles) * len(passes)
                for k in tiles:
                    for a, b in passes:
                        last = pe.matmul(dst, lhs[a](k), rhs[b](k), start=(n == 0), stop=(n == total - 1))
                        n += 1
                return last

            def sum_bias():
                pe.wait_ge(bias_ready, 1)
                pe.wait_ge(consts_loaded, 64)
                pe.wait_ge(w_loaded[3], 16)
                pe.wait_ge(fills_ready, 1)
                for j in range(KT):
                    pe.matmul(ctx_ps[0][:, 0:hidden], bv_rep[:, j, :], w_raw[3][:, j, :], start=(j == 0), stop=False)
                pe.matmul(ctx_ps[0][:, 0:hidden], ones_row[:, :], bf_row[:, :], start=False, stop=True)\
                    .then_inc(bias_summed, 1)

            def scores(b):
                g, cols = pair_of(b)
                wait(pe, qk_split, Batch(b.base, b.off // 2 * 2).count(plus=2))
                wait(pe, masked, b.count(per=HEADS))
                q, k = (qk_hi[:, g, 0, :, cols], qk_lo[:, g, 0, :, cols]), (qk_hi[:, g, 1, :, cols], qk_lo[:, g, 1, :, cols])
                for j in range(PAIRS):
                    for n, (a, c) in enumerate([(0, 1), (1, 0), (0, 0)]):
                        for r in range(2):
                            rows = slice(r * DH, (r + 1) * DH)
                            last = pe.matmul(score_ps[:, r, j * P:(j + 1) * P], q[a][rows, j, :], k[c][rows, j, :],
                                             start=(n == 0), stop=(n == 2))
                last.then_inc(scores_done, 1)

            def project(t, j):
                g, first = next_pair(t)
                c = t.off % 2
                if j == 0:
                    for b in (first, Batch(first.base, first.off + 1)):
                        wait(pe, h_turned[ring(b.off, 4)], b.dma_count(4, 16, 16))
                    wait(pe, proj_out, t.batch(2).count(per=KT))
                    if isinstance(t.base, int):
                        wait(pe, w_lo_ready, W_PLACE[c] + 1)
                elif j == 1:
                    wait(pe, v_split, t.batch(2).count())
                else:
                    wait(pe, proj_out, t.batch(2).count(per=KT, plus=1))
                product(proj_ps[j % 2][:, 0:2 * P],
                        [lambda k, w=w: w[c][:, k, j * P:(j + 1) * P] for w in (w_hi, w_lo)],
                        [lambda k, c=c: hT[:, g, c, k, :] for c in range(2)], range(KT)).then_inc(proj_done, 1)

            def project_v(b):
                g, cols = pair_of(b)
                if isinstance(b.base, int):
                    wait(pe, w_lo_ready, W_PLACE[2] + 1)
                wait(pe, proj_out, b.count(per=KT, plus=2))
                product(proj_ps[1][:, 0:hidden],
                        [lambda k, c=c: hT[:, g, c, k, cols] for c in range(2)],
                        [lambda k, w=w: w[2][:, k, :] for w in (w_hi, w_lo)], range(KT)).then_inc(v_done, 1)

            def attend(b):
                s, i = ring(b.off, 2), ring(b.off, X_RING)
                wait(pe, p_turned[s], b.dma_count(2, 16, 16))
                wait(pe, v_split, b.count(plus=1))
                wait(pe, ctx_split, b.count(plus=-1))
                if isinstance(b.base, int) and b.base + b.off == 0:
                    pe.wait_ge(bias_ready, 2)
                v = (v_hi, v_lo)
                for j in range(PAIRS):
                    for n, (a, c) in enumerate([(0, 1), (1, 0), (0, 0)]):
                        for r in range(2):
                            head = 2 * j + r
                            last = pe.matmul(ctx_ps[s][r * DH:(r + 1) * DH, j * P:(j + 1) * P],
                                             v[a][:, i, head * DH:(head + 1) * DH], pT[:, s, c, r * PAIRS + j, :],
                                             start=(n == 0), stop=(n == 2))
                last.then_inc(ctx_done, 1)

            def project_out(b):
                s = ring(b.off, 2)
                wait(pe, ctx_split, b.count(plus=1))
                wait(pe, out_ready, b.count(plus=-1))
                if isinstance(b.base, int):
                    wait(pe, w_lo_ready, W_PLACE[3] + 1)
                product(out_ps[s][:, 0:hidden], [lambda k, c=c: c[:, s, k, :] for c in (ctx_hi, ctx_lo)],
                        [lambda k, w=w: w[3][:, k, :] for w in (w_hi, w_lo)], range(KT)).then_inc(out_done, 1)

            def slot(t):
                projecting = t.batch(2).exists(batches)
                if projecting:
                    project(t, 0)
                b = t.batch(0)
                if b.exists(batches):
                    scores(b)
                b = t.batch(-2)
                if b.exists(batches):
                    attend(b)
                if projecting:
                    project(t, 1)
                    project(t, 2)
                b = t.batch(2)
                if b.exists(batches):
                    project_v(b)
                b = t.batch(-2)
                if b.exists(batches):
                    project_out(b)

            slots(pe, batches, slot, {-2: sum_bias})


_INS = ["x", "adj", "L0_gnn_Wq", "L0_gnn_bq", "L0_gnn_Wk", "L0_gnn_bk", "L0_gnn_Wv", "L0_gnn_bv", "L0_gnn_Wf", "L0_gnn_bf"]


def kernel(**inputs):
    import numpy as _np
    import concourse.bacc as _bacc
    from concourse import mybir as _mybir
    from concourse.bass_utils import run_bass_kernel_spmd as _run

    nc = _bacc.Bacc("TRN2", target_bir_lowering=False, num_devices=1)
    arrays, args = {}, []
    for name in _INS:
        a = _np.ascontiguousarray(inputs[name])
        arrays[f"in_{name}_dram"] = a
        args.append(nc.dram_tensor(f"in_{name}_dram", a.shape, _mybir.dt.from_np(a.dtype), kind="ExternalInput").ap())
    x = arrays["in_x_dram"]
    out = nc.dram_tensor("out_dram", x.shape, _mybir.dt.float32, kind="ExternalOutput").ap()
    graph_attention(nc, *args, out)
    r = _run(nc, [arrays], core_ids=[0])
    return r.results[0]["out_dram"]
```

```python
import concourse.bass as bass
from concourse import mybir

F32 = mybir.dt.float32
F16 = mybir.dt.float16
U8 = mybir.dt.uint8
U32 = mybir.dt.uint32
ALU = mybir.AluOpType
ACT = mybir.ActivationFunctionType
AX = mybir.AxisListType

P = 128
HEADS = 6
DH = 64
EPS = 1e-5
NEG = -9000000000000000.0

H_SCALE = 2.0 ** 11
PROJ_SCALE = 2.0 ** -19
QKV_EXP = -8
PROB_SCALE = 2.0 ** 15
W_TARGET = 2.0 ** 13
W_FLOOR = 2.0 ** -26

UNROLL = 8
LAST_LAG = 3
FIRST_SLOT = -4
EARLY = 4


def ring(b, n):
    return b % n


class Step:

    def __init__(self, base, off):
        self.base, self.off = base, off

    def left(self, batches):
        return batches - 1 - (self.base + self.off) if isinstance(self.base, int) else UNROLL

    def batch(self, lag):
        return Batch(self.base, self.off + lag)


class Batch:
    def __init__(self, base, off):
        self.base, self.off = base, off

    def exists(self, batches):
        return not isinstance(self.base, int) or 0 <= self.base + self.off < batches

    def early(self):
        return isinstance(self.base, int) and self.base + self.off < EARLY

    def count(self, per=1, plus=0):
        return self.base * per + (self.off * per + plus)

    def dma_count(self, n, per, plus=0):
        if isinstance(self.base, int):
            return (self.base + self.off) // n * per + plus
        return self.base * (per // n) + (self.off // n * per + plus)


def wait(eng, sem, value):
    if not isinstance(value, int) or value > 0:
        eng.wait_ge(sem, value)


def apart(eng):
    eng.nop(nofuse=True)


def slots(eng, batches, body):
    for t in range(FIRST_SLOT, UNROLL):
        body(Step(0, t))
    with eng.Fori(1, batches // UNROLL - 1) as n:
        for off in range(UNROLL):
            body(Step(n * UNROLL, off))
    for off in range(UNROLL + LAST_LAG):
        body(Step(batches - UNROLL, off))


def graph_attention(nc, x, adj, Wq, bq, Wk, bk, Wv, bv, Wf, bf, out):
    batches, tokens, hidden = x.shape
    assert tokens == P and hidden == HEADS * DH and batches % UNROLL == 0 and batches >= 2 * UNROLL
    KT = hidden // P
    PAIRS = HEADS // 2
    assert PAIRS == KT

    from contextlib import ExitStack
    with ExitStack() as ctx:
        def sb(name, shape, dt=F32):
            return ctx.enter_context(nc.sbuf_tensor(name, shape, dt))

        def bank(name):
            return ctx.enter_context(nc.psum_tensor(name, [P, 512], F32))

        def sem(name):
            return ctx.enter_context(nc.semaphore(name))

        ones_row = sb("ones_row", [1, P])
        w_raw = [sb(f"w_raw_{n}", [P, KT, hidden]) for n in "qkvf"]
        w_hi = [sb(f"w_hi_{n}", [P, KT, hidden], F16) for n in "qkvf"]
        w_lo = [sb(f"w_lo_{n}", [P, KT, hidden], F16) for n in "qkvf"]
        extremes = sb("extremes", [P, 10])
        ext_all = sb("ext_all", [P, 10])
        bias_max = sb("bias_max", [P, 2])
        top = sb("top", [P, 4])
        top_pow = sb("top_pow", [P, 4])
        top_floor = sb("top_floor", [P, 4])
        top_rec = sb("top_rec", [P, 4])
        w_scale = sb("w_scale", [P, 4])
        pair_pow = sb("pair_pow", [P, 2])
        pair_scale = sb("pair_scale", [P, 1])
        score_scale = sb("score_scale", [P, 1])
        out_scale = sb("out_scale", [P, 1])
        mask_scale = sb("mask_scale", [P, 2])
        qk_bias = sb("qk_bias", [P, 2, KT])
        bv_col = sb("bv_col", [P, KT])
        bv_rep = sb("bv_rep", [P, KT, P])
        bf_row = sb("bf_row", [1, hidden])
        out_bias = sb("out_bias", [P, hidden])

        X_RING, IO = 8, 4
        x_sb = sb("x_sb", [P, X_RING, hidden])
        adj_sb = sb("adj_sb", [P, X_RING, P], U8)
        stats = sb("stats", [P, 2, 6])
        mean_var = sb("mean_var", [P, 2, 2])
        var_eps = sb("var_eps", [P, 2, 1])
        neg_mean = sb("neg_mean", [P, 2, 1])
        rstd = sb("rstd", [P, 2, 1])
        half_power = sb("half_power", [P, 1])
        resid = sb("resid", [P, X_RING, hidden])
        xn = sb("xn", [P, 2, hidden])
        h_parts = sb("h_parts", [P, 2, 2, hidden], F16)
        hT = sb("hT", [P, 2, 2, KT, 2 * P], F16)
        qk_full = sb("qk_full", [P, 2, KT, 2 * P])
        qk_hi = sb("qk_hi", [P, 2, 2, KT, 2 * P], F16)
        qk_lo = sb("qk_lo", [P, 2, 2, KT, 2 * P], F16)
        v_hi = sb("v_hi", [P, X_RING, hidden], F16)
        v_lo = sb("v_lo", [P, X_RING, hidden], F16)
        mask = sb("mask", [P, 2, P])
        neg_scores = sb("neg_scores", [P, 2, HEADS, P])
        neg_max = sb("neg_max", [P, 2, HEADS])
        probs = sb("probs", [P, 2, HEADS, P])
        sums = sb("sums", [P, 2, HEADS])
        inv_sums = sb("inv_sums", [P, 2, HEADS])
        probs_n = sb("probs_n", [P, 2, HEADS, P])
        p_parts = sb("p_parts", [P, 2, 2, HEADS, P], F16)
        pT = sb("pT", [P, 2, 2, HEADS, P], F16)
        ctx_hi = sb("ctx_hi", [P, 2, KT, P], F16)
        ctx_lo = sb("ctx_lo", [P, 2, KT, P], F16)
        out_sb = sb("out_sb", [P, IO, hidden])

        score_ps = ctx.enter_context(nc.psum_tensor("score_ps", [P, 2, 512], F32))
        ctx_ps = [bank("ctx_ps0"), bank("ctx_ps1")]
        out_ps = [bank("out_ps0"), bank("out_ps1")]
        proj_ps = [bank("proj_ps0"), bank("proj_ps1")]

        vf_bias_loaded = sem("vf_bias_loaded")
        qk_bias_loaded = sem("qk_bias_loaded")
        w_loaded = [sem(f"w_loaded_{n}") for n in "qkvf"]
        loaded = [sem(f"loaded{i}") for i in range(IO)]
        stored = [sem(f"stored{i}") for i in range(IO)]
        fills_ready = sem("fills_ready")
        ext_ready = sem("ext_ready")
        ext_reduced = sem("ext_reduced")
        setup_step = sem("setup_step")
        w_hi_ready = sem("w_hi_ready")
        w_lo_ready = sem("w_lo_ready")
        bias_summed = sem("bias_summed")
        bias_ready = sem("bias_ready")
        stats_done = sem("stats_done")
        ln_step = sem("ln_step")
        xn_ready = sem("xn_ready")
        resid_ready = sem("resid_ready")
        h_hi_ready = sem("h_hi_ready")
        h_split = sem("h_split")
        h_turned = [sem(f"h_turned{i}") for i in range(4)]
        proj_done = sem("proj_done")
        proj_out = sem("proj_out")
        qk_hi_ready = sem("qk_hi_ready")
        qk_split = sem("qk_split")
        v_done = sem("v_done")
        v_hi_ready = sem("v_hi_ready")
        v_split = sem("v_split")
        mask_ready = sem("mask_ready")
        scores_done = sem("scores_done")
        masked = sem("masked")
        exp_done = sem("exp_done")
        inverted = sem("inverted")
        normed = sem("normed")
        p_hi_ready = sem("p_hi_ready")
        p_split = sem("p_split")
        p_turned = [sem(f"p_turned{i}") for i in range(2)]
        ctx_done = sem("ctx_done")
        ctx_hi_ready = sem("ctx_hi_ready")
        ctx_split = sem("ctx_split")
        out_done = sem("out_done")
        out_ready = sem("out_ready")

        W_ORDER = (0, 2, 1, 3)
        W_PLACE = {n: i for i, n in enumerate(W_ORDER)}

        block = ctx.enter_context(nc.Block())

        def pair_of(b):
            o = b.off
            return o // 2 % 2, slice(o % 2 * P, (o % 2 + 1) * P)

        def next_pair(t):
            b = Batch(t.base, t.off // 2 * 2 + 2)
            return b.off // 2 % 2, b

        @block.sync
        def _(sp):
            def load(b):
                i = ring(b.off, X_RING)
                wait(sp, resid_ready, b.count(plus=1 - X_RING))
                apart(sp)
                wait(sp, mask_ready, b.count(plus=1 - X_RING))
                apart(sp)
                wait(sp, xn_ready, b.count(plus=1 - IO))
                apart(sp)
                got = loaded[ring(b.off, IO)]
                if isinstance(b.base, int):
                    src_x, src_adj = x[b.base + b.off], adj[b.base + b.off]
                else:
                    n = b.base + b.off
                    src_x = x[bass.ds(n, 1)].rearrange("o p h -> (o p) h")
                    src_adj = adj[bass.ds(n, 1)].rearrange("o p h -> (o p) h")
                sp.dma_start(x_sb[:, i, :], src_x).then_inc(got, 16)
                sp.dma_start(adj_sb[:, i, :], src_adj).then_inc(got, 16)

            def store(b):
                wait(sp, out_ready, b.count(plus=1))
                apart(sp)
                if isinstance(b.base, int):
                    dst = out[b.base + b.off]
                else:
                    dst = out[bass.ds(b.base + b.off, 1)].rearrange("o p h -> (o p) h")
                sp.dma_start(dst, out_sb[:, ring(b.off, IO), :]).then_inc(stored[ring(b.off, IO)], 16)

            def load_weight(n, W):
                sp.dma_start(w_raw[n][:, :, :], W.rearrange("(t p) n -> p t n", p=P)).then_inc(w_loaded[n], 16)

            def load_column(dst, b, got):
                sp.dma_start(dst, b.rearrange("(t p) -> p t", p=P), allow_slow_non_contiguous=True)\
                    .then_inc(got, 16)

            load(Batch(0, 0))
            load(Batch(0, 1))
            load_weight(0, Wq)
            load(Batch(0, 2))
            load_weight(2, Wv)
            load_column(extremes[:, 4:4 + KT], bq, qk_bias_loaded)
            load_column(extremes[:, 4 + KT:4 + 2 * KT], bk, qk_bias_loaded)
            load_weight(1, Wk)
            load_column(bv_col[:, :], bv, vf_bias_loaded)
            load_weight(3, Wf)
            sp.dma_start(bf_row[:, :], bf.rearrange("(o n) -> o n", o=1)).then_inc(vf_bias_loaded, 16)
            load(Batch(0, 3))

            def turn_h(b):
                g, cols = pair_of(b)
                wait(sp, h_split, b.count(plus=1))
                apart(sp)
                wait(sp, v_done, Batch(b.base, b.off // 2 * 2).count(plus=-2))
                apart(sp)
                sp.dma_start_transpose(hT[:, g, :, :, cols].rearrange("p c j q -> p (c j) q"),
                                       h_parts[:, ring(b.off, 2), :, :].rearrange("p c n -> p (c n)"))\
                    .then_inc(h_turned[ring(b.off, 4)], 16)

            def turn_p(b):
                s = ring(b.off, 2)
                wait(sp, p_split, b.count(plus=1))
                apart(sp)
                wait(sp, ctx_done, b.count(plus=-1))
                apart(sp)
                sp.dma_start_transpose(pT[:, s, :, :, :].rearrange("p c h q -> p (c h) q"),
                                       p_parts[:, s, :, :, :].rearrange("p c h k -> p (c h k)"))\
                    .then_inc(p_turned[s], 16)

            def slot(t):
                b = t.batch(6)
                if b.exists(batches) and not b.early():
                    load(b)
                b = t.batch(4)
                if b.exists(batches):
                    turn_h(b)
                done, turned = t.batch(-3), t.batch(-1)
                if done.exists(batches) and t.left(batches) >= 1:
                    store(done)
                if turned.exists(batches):
                    turn_p(turned)
                if done.exists(batches) and t.left(batches) < 1:
                    store(done)

            slots(sp, batches, slot)
            for i in range(IO):
                sp.wait_ge(stored[i], 16 * (batches // IO))

        @block.gpsimd
        def _(pool):
            pool.memset(ones_row[:, :], 1.0).then_inc(fills_ready, 1)
            pool.memset(half_power[:, :], -0.5).then_inc(fills_ready, 1)
            pool.wait_ge(fills_ready, 2)

            def reduce_extremes():
                pool.wait_ge(ext_ready, 4)
                pool.wait_ge(qk_bias_loaded, 32)
                pool.partition_all_reduce(ext_all[:, :], extremes[:, :], P, bass.bass_isa.ReduceOp.absmax)\
                    .then_inc(ext_reduced, 1)

            def make_mask(b):
                wait(pool, masked, b.count(per=HEADS, plus=-HEADS))
                if isinstance(b.base, int) and b.base + b.off == 0:
                    pool.wait_ge(setup_step, 11)
                apart(pool)
                pool.tensor_scalar(mask[:, ring(b.off, 2), :], adj_sb[:, ring(b.off, X_RING), :],
                                   mask_scale[:, 0:1], mask_scale[:, 1:2], ALU.mult, ALU.add)\
                    .then_inc(mask_ready, 1)

            def layer_norm(b):
                s = ring(b.off, 2)
                xb = x_sb[:, ring(b.off, X_RING), :]
                wait(pool, loaded[ring(b.off, IO)], b.dma_count(IO, 32, 32))
                wait(pool, stats_done, b.count(per=2, plus=2))
                apart(pool)
                pool.tensor_scalar(var_eps[:, s, :], mean_var[:, s, 1:2], EPS, H_SCALE ** -2, ALU.add, ALU.mult)\
                    .then_inc(ln_step, 1)
                pool.tensor_scalar(neg_mean[:, s, :], mean_var[:, s, 0:1], -1.0, 0.0, ALU.mult, ALU.add)\
                    .then_inc(ln_step, 1)
                wait(pool, ln_step, b.count(per=3, plus=2))
                pool.tensor_tensor(rstd[:, s, :], var_eps[:, s, :], half_power[:, :], ALU.pow).then_inc(ln_step, 1)
                wait(pool, ln_step, b.count(per=3, plus=3))
                wait(pool, h_split, b.count(plus=-1))
                apart(pool)
                pool.tensor_scalar(xn[:, s, :], xb, neg_mean[:, s, :], rstd[:, s, :],
                                   ALU.add, ALU.mult).then_inc(xn_ready, 1)

            def residual(b):
                i = ring(b.off, X_RING)
                if isinstance(b.base, int) and b.base + b.off == 0:
                    pool.wait_ge(bias_ready, 2)
                wait(pool, out_ready, b.count(plus=1 - X_RING))
                pool.tensor_tensor(resid[:, i, :], x_sb[:, i, :], out_bias[:, :], ALU.add).then_inc(resid_ready, 1)

            def qk_low(t):
                g, first = next_pair(t)
                c = t.off % 2
                wait(pool, qk_hi_ready, t.batch(2).count(plus=1))
                wait(pool, scores_done, first.count(plus=-2))
                pool.tensor_tensor(qk_lo[:, g, c, :, :], qk_full[:, c, :, :], qk_hi[:, g, c, :, :], ALU.subtract)\
                    .then_inc(qk_split, 1)

            def normalise(b):
                s = ring(b.off, 2)
                wait(pool, exp_done, b.count(per=HEADS, plus=HEADS))
                wait(pool, inverted, b.count(plus=1))
                wait(pool, p_split, b.count(plus=-1))
                pool.tensor_tensor(probs_n[:, s, :, :], probs[:, s, :, :],
                                   inv_sums[:, s, :].unsqueeze(2).to_broadcast([P, HEADS, P]), ALU.mult)\
                    .then_inc(normed, 1)

            def slot(t):
                b = t.batch(-1)
                if b.exists(batches):
                    normalise(b)
                b = t.batch(5)
                if b.exists(batches) and not b.early():
                    layer_norm(b)
                b = t.batch(1)
                if b.exists(batches):
                    make_mask(b)
                if t.batch(2).exists(batches):
                    first = isinstance(t.base, int) and t.base == 0 and t.off < 0
                    if first:
                        qk_low(t)
                    residual(t.batch(2))
                    if not first:
                        qk_low(t)

            for b in range(EARLY - 1):
                layer_norm(Batch(0, b))
            reduce_extremes()
            layer_norm(Batch(0, EARLY - 1))
            slots(pool, batches, slot)

        @block.scalar
        def _(act):
            def weight_high(n):
                act.wait_ge(w_loaded[n], 16)
                act.activation(w_hi[n][:, :, :], w_raw[n][:, :, :], ACT.Copy, scale=w_scale[:, n:n + 1])\
                    .then_inc(w_hi_ready, 1)

            def qk_out(t, j):
                c = t.off % 2
                b = t.batch(2)
                wait(act, proj_done, b.count(per=KT, plus=j + 1))
                if j == 0:
                    wait(act, qk_split, b.count(plus=-1))
                    if isinstance(t.base, int) and b.base + b.off == 0:
                        act.wait_ge(setup_step, 13)
                act.activation(qk_full[:, c, j, :], proj_ps[j % 2][:, 0:2 * P], ACT.Identity,
                               bias=qk_bias[:, c, j:j + 1], scale=PROJ_SCALE).then_inc(proj_out, 1)

            def exps(b, heads):
                s = ring(b.off, 2)
                for h in heads:
                    if h == 0:
                        wait(act, normed, b.count(plus=-1))
                    wait(act, masked, b.count(per=HEADS, plus=h + 1))
                    act.activation(probs[:, s, h, :], neg_scores[:, s, h, :], ACT.Exp, scale=-1.0,
                                   bias=neg_max[:, s, h:h + 1], accum_out=sums[:, s, h:h + 1])\
                        .then_inc(exp_done, 1)

            def ctx_high(b):
                wait(act, ctx_done, b.count(plus=1))
                wait(act, out_done, b.count(plus=-1))
                act.activation(ctx_hi[:, ring(b.off, 2), :, :], ctx_ps[ring(b.off, 2)][:, 0:hidden].rearrange("p (j q) -> p j q", j=KT),
                               ACT.Copy, scale=1.0 / PROB_SCALE).then_inc(ctx_hi_ready, 1)

            def p_high(b):
                s = ring(b.off, 2)
                wait(act, normed, b.count(plus=1))
                wait(act, p_turned[s], b.dma_count(2, 16))
                act.activation(p_parts[:, s, 0, :, :], probs_n[:, s, :, :], ACT.Copy, scale=PROB_SCALE)\
                    .then_inc(p_hi_ready, 1)

            def v_high(b):
                wait(act, v_done, b.count(plus=1))
                wait(act, ctx_done, b.count(plus=1 - X_RING))
                act.activation(v_hi[:, ring(b.off, X_RING), :], proj_ps[1][:, 0:hidden], ACT.Copy,
                               scale=PROJ_SCALE).then_inc(v_hi_ready, 1)

            def h_high(b):
                s = ring(b.off, 2)
                wait(act, xn_ready, b.count(plus=1))
                two_back = Batch(b.base, b.off - 2)
                if two_back.exists(batches):
                    wait(act, h_turned[ring(two_back.off, 4)], two_back.dma_count(4, 16, 16))
                act.activation(h_parts[:, s, 0, :], xn[:, s, :], ACT.Relu).then_inc(h_hi_ready, 1)

            def slot(t):
                scored, used, turned, coming = t.batch(0), t.batch(-2), t.batch(-1), t.batch(5)
                projecting = t.batch(2).exists(batches)
                if projecting:
                    qk_out(t, 0)
                if t.left(batches) == 0:
                    exps(scored, range(HEADS))
                    p_high(turned)
                else:
                    if turned.exists(batches):
                        p_high(turned)
                    if scored.exists(batches):
                        exps(scored, range(0, PAIRS))
                if projecting:
                    qk_out(t, 1)
                if used.exists(batches):
                    ctx_high(used)
                if projecting:
                    qk_out(t, 2)
                if scored.exists(batches) and t.left(batches) > 0:
                    exps(scored, range(PAIRS, HEADS))
                if coming.exists(batches) and not coming.early():
                    h_high(coming)
                if projecting:
                    v_high(t.batch(2))

            for b in range(EARLY - 1):
                h_high(Batch(0, b))
            act.wait_ge(setup_step, 7)
            weight_high(W_ORDER[0])
            h_high(Batch(0, EARLY - 1))
            for n in W_ORDER[1:]:
                weight_high(n)
            slots(act, batches, slot)

        @block.vector
        def _(dve):
            def maximum(n):
                dve.wait_ge(w_loaded[n], 16)
                dve.tensor_reduce(extremes[:, n:n + 1], w_raw[n][:, :, :], AX.XY, ALU.max,
                                  apply_absolute_value=True).then_inc(ext_ready, 1)

            def repeat_bv():
                dve.wait_ge(vf_bias_loaded, 32)
                for j in range(KT):
                    last = dve.tensor_copy(bv_rep[:, j, :], bv_col[:, j:j + 1].to_broadcast([P, P]))
                last.then_inc(bias_ready, 1)

            def setup_scales():
                dve.wait_ge(ext_reduced, 1)
                dve.tensor_reduce(bias_max[:, :], ext_all[:, 4:10].rearrange("p (c t) -> p c t", c=2), AX.X, ALU.max)\
                    .then_inc(setup_step, 1)
                dve.tensor_scalar(top[:, 2:4], ext_all[:, 2:4], W_FLOOR, None, ALU.max).then_inc(setup_step, 1)
                dve.wait_ge(setup_step, 2)
                dve.scalar_tensor_tensor(out=top[:, 0:2], in0=bias_max[:, :], scalar=2.0 ** QKV_EXP, in1=ext_all[:, 0:2],
                                         op0=ALU.mult, op1=ALU.max).then_inc(setup_step, 1)
                dve.wait_ge(setup_step, 3)
                dve.tensor_scalar(top_floor[:, :], top[:, :], W_FLOOR, None, ALU.max).then_inc(setup_step, 1)
                dve.wait_ge(setup_step, 4)
                dve.tensor_scalar(top_pow[:, :].bitcast(U32), top_floor[:, :].bitcast(U32), 0x7f800000, None,
                                  ALU.bitwise_and).then_inc(setup_step, 1)
                dve.wait_ge(setup_step, 5)
                dve.reciprocal(top_rec[:, :], top_pow[:, :]).then_inc(setup_step, 1)
                dve.wait_ge(setup_step, 6)
                dve.tensor_scalar(w_scale[:, :], top_rec[:, :], W_TARGET, None, ALU.mult).then_inc(setup_step, 1)
                dve.wait_ge(setup_step, 7)
                pows = top_pow[:, :].rearrange("p (c t) -> p c t", t=2)
                dve.tensor_tensor(pair_pow[:, :], pows[:, :, 0], pows[:, :, 1], ALU.mult).then_inc(setup_step, 1)
                dve.tensor_tensor(pair_scale[:, :], w_scale[:, 0:1], w_scale[:, 1:2], ALU.mult).then_inc(setup_step, 1)
                dve.wait_ge(setup_step, 9)
                dve.tensor_scalar(mask_scale[:, 0:1], pair_scale[:, :], -NEG * 8.0 * 2.0 ** (2 * QKV_EXP), None, ALU.mult)\
                    .then_inc(setup_step, 1)
                dve.tensor_scalar(mask_scale[:, 1:2], pair_scale[:, :], NEG * 8.0 * 2.0 ** (2 * QKV_EXP), None, ALU.mult)\
                    .then_inc(setup_step, 1)
                for c in range(2):
                    dve.tensor_scalar(qk_bias[:, c, :], extremes[:, 4 + KT * c:4 + KT * (c + 1)], w_scale[:, c:c + 1],
                                      2.0 ** QKV_EXP, ALU.mult, ALU.mult).then_inc(setup_step, 1)
                dve.tensor_scalar(score_scale[:, :], pair_pow[:, 0:1], -(W_TARGET * 2.0 ** QKV_EXP) ** -2 / 8.0, None,
                                  ALU.mult).then_inc(setup_step, 1)
                dve.tensor_scalar(out_scale[:, :], pair_pow[:, 1:2], W_TARGET ** -2 * 2.0 ** -QKV_EXP, None,
                                  ALU.mult).then_inc(setup_step, 1)

            def weight_low(n):
                dve.wait_ge(w_hi_ready, W_PLACE[n] + 1)
                dve.scalar_tensor_tensor(out=w_lo[n][:, :, :], in0=w_raw[n][:, :, :], scalar=w_scale[:, n:n + 1],
                                         in1=w_hi[n][:, :, :], op0=ALU.mult, op1=ALU.subtract)\
                    .then_inc(w_lo_ready, 1)

            def copy_bias():
                dve.wait_ge(bias_summed, 1)
                dve.tensor_copy(out_bias[:, :], ctx_ps[0][:, 0:hidden]).then_inc(bias_ready, 1)
                dve.wait_ge(setup_step, 15)

            def mask_scores(b):
                s = ring(b.off, 2)
                wait(dve, scores_done, b.count(plus=1))
                wait(dve, mask_ready, b.count(plus=1))
                wait(dve, exp_done, b.count(per=HEADS, plus=-HEADS))
                apart(dve)
                for r in range(2):
                    for j in range(PAIRS):
                        h = r * PAIRS + j
                        dve.tensor_tensor_reduce(neg_scores[:, s, h, :], score_ps[:, r, j * P:(j + 1) * P],
                                                 mask[:, s, :], score_scale[:, :], 3.0e38, ALU.add, ALU.min,
                                                 neg_max[:, s, h:h + 1]).then_inc(masked, 1)

            def ctx_low(b):
                s = ring(b.off, 2)
                wait(dve, ctx_hi_ready, b.count(plus=1))
                dve.scalar_tensor_tensor(out=ctx_lo[:, s, :, :], in0=ctx_ps[ring(b.off, 2)][:, 0:hidden].rearrange("p (j q) -> p j q", j=KT),
                                         scalar=1.0 / PROB_SCALE, in1=ctx_hi[:, s, :, :], op0=ALU.mult,
                                         op1=ALU.subtract).then_inc(ctx_split, 1)

            def statistics(b):
                s = ring(b.off, 2)
                wait(dve, loaded[ring(b.off, IO)], b.dma_count(IO, 32, 32))
                wait(dve, xn_ready, b.count(plus=-1))
                dve.bn_stats(stats[:, s, :], x_sb[:, ring(b.off, X_RING), :]).then_inc(stats_done, 1)
                wait(dve, stats_done, b.count(per=2, plus=1))
                apart(dve)
                dve.bn_aggr(mean_var[:, s, :], stats[:, s, :]).then_inc(stats_done, 1)

            def qk_high(t):
                g, first = next_pair(t)
                c = t.off % 2
                wait(dve, proj_out, t.batch(2).count(per=KT, plus=KT))
                wait(dve, scores_done, first.count(plus=-2))
                dve.tensor_copy(qk_hi[:, g, c, :, :], qk_full[:, c, :, :]).then_inc(qk_hi_ready, 1)

            def invert(b):
                s = ring(b.off, 2)
                wait(dve, exp_done, b.count(per=HEADS, plus=HEADS))
                wait(dve, normed, b.count(plus=-1))
                dve.reciprocal(inv_sums[:, s, :], sums[:, s, :]).then_inc(inverted, 1)

            def p_low(b):
                s = ring(b.off, 2)
                wait(dve, p_hi_ready, b.count(plus=1))
                dve.scalar_tensor_tensor(out=p_parts[:, s, 1, :, :], in0=probs_n[:, s, :, :], scalar=PROB_SCALE,
                                         in1=p_parts[:, s, 0, :, :], op0=ALU.mult, op1=ALU.subtract)\
                    .then_inc(p_split, 1)

            def finish(b):
                wait(dve, out_done, b.count(plus=1))
                wait(dve, resid_ready, b.count(plus=1))
                wait(dve, stored[ring(b.off, IO)], b.dma_count(IO, 16))
                dve.scalar_tensor_tensor(out=out_sb[:, ring(b.off, IO), :], in0=out_ps[ring(b.off, 2)][:, 0:hidden],
                                         scalar=out_scale[:, :], in1=resid[:, ring(b.off, X_RING), :],
                                         op0=ALU.mult, op1=ALU.add).then_inc(out_ready, 1)

            def v_low(b):
                i = ring(b.off, X_RING)
                wait(dve, v_hi_ready, b.count(plus=1))
                dve.scalar_tensor_tensor(out=v_lo[:, i, :], in0=proj_ps[1][:, 0:hidden], scalar=PROJ_SCALE,
                                         in1=v_hi[:, i, :], op0=ALU.mult, op1=ALU.subtract).then_inc(v_split, 1)

            def h_low(b):
                s = ring(b.off, 2)
                wait(dve, h_hi_ready, b.count(plus=1))
                dve.scalar_tensor_tensor(out=h_parts[:, s, 1, :], in0=xn[:, s, :], scalar=0.0,
                                         in1=h_parts[:, s, 0, :], op0=ALU.max, op1=ALU.subtract)\
                    .then_inc(h_split, 1)

            def slot(t):
                b = t.batch(5)
                if b.exists(batches) and not b.early():
                    statistics(b)
                scored, turned, used, coming = t.batch(0), t.batch(-1), t.batch(-2), t.batch(2)
                if scored.exists(batches):
                    mask_scores(scored)
                if scored.exists(batches) and t.left(batches) < 1:
                    invert(scored)
                if turned.exists(batches):
                    p_low(turned)
                if used.exists(batches):
                    ctx_low(used)
                if t.left(batches) < 1:
                    finish(t.batch(-3))
                if coming.exists(batches):
                    qk_high(t)
                if scored.exists(batches) and t.left(batches) >= 1:
                    invert(scored)
                if coming.exists(batches):
                    v_low(coming)
                    if used.exists(batches):
                        finish(used)
                b = t.batch(5)
                if b.exists(batches) and not b.early():
                    h_low(b)

            statistics(Batch(0, 0))
            statistics(Batch(0, 1))
            h_low(Batch(0, 0))
            maximum(0)
            statistics(Batch(0, 2))
            h_low(Batch(0, 1))
            maximum(2)
            maximum(1)
            repeat_bv()
            maximum(3)
            statistics(Batch(0, 3))
            setup_scales()
            for n in W_ORDER[:2]:
                weight_low(n)
            h_low(Batch(0, 2))
            h_low(Batch(0, 3))
            for n in W_ORDER[2:]:
                weight_low(n)
            copy_bias()
            slots(dve, batches, slot)

        @block.tensor
        def _(pe):
            def product(dst, lhs, rhs, tiles, start=True):
                passes = [(0, 1), (1, 0), (0, 0)]
                n, total = 0, len(tiles) * len(passes)
                for k in tiles:
                    for a, b in passes:
                        last = pe.matmul(dst, lhs[a](k), rhs[b](k), start=(n == 0), stop=(n == total - 1))
                        n += 1
                return last

            def sum_bias():
                pe.wait_ge(bias_ready, 1)
                pe.wait_ge(vf_bias_loaded, 32)
                pe.wait_ge(w_loaded[3], 16)
                pe.wait_ge(fills_ready, 1)
                for j in range(KT):
                    pe.matmul(ctx_ps[0][:, 0:hidden], bv_rep[:, j, :], w_raw[3][:, j, :], start=(j == 0), stop=False)
                pe.matmul(ctx_ps[0][:, 0:hidden], ones_row[:, :], bf_row[:, :], start=False, stop=True)\
                    .then_inc(bias_summed, 1)

            def scores(b):
                g, cols = pair_of(b)
                wait(pe, qk_split, Batch(b.base, b.off // 2 * 2).count(plus=2))
                wait(pe, masked, b.count(per=HEADS))
                q, k = (qk_hi[:, g, 0, :, cols], qk_lo[:, g, 0, :, cols]), (qk_hi[:, g, 1, :, cols], qk_lo[:, g, 1, :, cols])
                for j in range(PAIRS):
                    for n, (a, c) in enumerate([(0, 1), (1, 0), (0, 0)]):
                        for r in range(2):
                            rows = slice(r * DH, (r + 1) * DH)
                            last = pe.matmul(score_ps[:, r, j * P:(j + 1) * P], q[a][rows, j, :], k[c][rows, j, :],
                                             start=(n == 0), stop=(n == 2))
                last.then_inc(scores_done, 1)

            def project(t, j):
                g, first = next_pair(t)
                c = t.off % 2
                if j == 0:
                    for b in (first, Batch(first.base, first.off + 1)):
                        wait(pe, h_turned[ring(b.off, 4)], b.dma_count(4, 16, 16))
                    wait(pe, proj_out, t.batch(2).count(per=KT))
                    if isinstance(t.base, int):
                        wait(pe, w_lo_ready, W_PLACE[c] + 1)
                elif j == 1:
                    wait(pe, v_split, t.batch(2).count())
                else:
                    wait(pe, proj_out, t.batch(2).count(per=KT, plus=1))
                product(proj_ps[j % 2][:, 0:2 * P],
                        [lambda k, w=w: w[c][:, k, j * P:(j + 1) * P] for w in (w_hi, w_lo)],
                        [lambda k, c=c: hT[:, g, c, k, :] for c in range(2)], range(KT)).then_inc(proj_done, 1)

            def project_v(b):
                g, cols = pair_of(b)
                if isinstance(b.base, int):
                    wait(pe, w_lo_ready, W_PLACE[2] + 1)
                wait(pe, proj_out, b.count(per=KT, plus=2))
                product(proj_ps[1][:, 0:hidden],
                        [lambda k, c=c: hT[:, g, c, k, cols] for c in range(2)],
                        [lambda k, w=w: w[2][:, k, :] for w in (w_hi, w_lo)], range(KT)).then_inc(v_done, 1)

            def attend(b):
                s, i = ring(b.off, 2), ring(b.off, X_RING)
                wait(pe, p_turned[s], b.dma_count(2, 16, 16))
                wait(pe, v_split, b.count(plus=1))
                wait(pe, ctx_split, b.count(plus=-1))
                if isinstance(b.base, int) and b.base + b.off == 0:
                    pe.wait_ge(bias_ready, 2)
                v = (v_hi, v_lo)
                for j in range(PAIRS):
                    for n, (a, c) in enumerate([(0, 1), (1, 0), (0, 0)]):
                        for r in range(2):
                            head = 2 * j + r
                            last = pe.matmul(ctx_ps[s][r * DH:(r + 1) * DH, j * P:(j + 1) * P],
                                             v[a][:, i, head * DH:(head + 1) * DH], pT[:, s, c, r * PAIRS + j, :],
                                             start=(n == 0), stop=(n == 2))
                last.then_inc(ctx_done, 1)

            def project_out(b):
                s = ring(b.off, 2)
                wait(pe, ctx_split, b.count(plus=1))
                wait(pe, out_ready, b.count(plus=-1))
                if isinstance(b.base, int):
                    wait(pe, w_lo_ready, W_PLACE[3] + 1)
                product(out_ps[s][:, 0:hidden], [lambda k, c=c: c[:, s, k, :] for c in (ctx_hi, ctx_lo)],
                        [lambda k, w=w: w[3][:, k, :] for w in (w_hi, w_lo)], range(KT)).then_inc(out_done, 1)

            def slot(t):
                projecting = t.batch(2).exists(batches)
                if projecting:
                    project(t, 0)
                b = t.batch(0)
                if b.exists(batches):
                    scores(b)
                if projecting:
                    project(t, 1)
                elif t.left(batches) < 1:
                    project_out(t.batch(-3))
                b = t.batch(-2)
                if b.exists(batches):
                    attend(b)
                if projecting:
                    project(t, 2)
                b = t.batch(2)
                if b.exists(batches):
                    project_v(b)
                b = t.batch(-2)
                if projecting and b.exists(batches):
                    project_out(b)

            sum_bias()
            slots(pe, batches, slot)


_INS = ["x", "adj", "L0_gnn_Wq", "L0_gnn_bq", "L0_gnn_Wk", "L0_gnn_bk", "L0_gnn_Wv", "L0_gnn_bv", "L0_gnn_Wf", "L0_gnn_bf"]


def kernel(**inputs):
    import numpy as _np
    import concourse.bacc as _bacc
    from concourse import mybir as _mybir
    from concourse.bass_utils import run_bass_kernel_spmd as _run

    nc = _bacc.Bacc("TRN2", target_bir_lowering=False, num_devices=1)
    arrays, args = {}, []
    for name in _INS:
        a = _np.ascontiguousarray(inputs[name])
        arrays[f"in_{name}_dram"] = a
        args.append(nc.dram_tensor(f"in_{name}_dram", a.shape, _mybir.dt.from_np(a.dtype), kind="ExternalInput").ap())
    x = arrays["in_x_dram"]
    out = nc.dram_tensor("out_dram", x.shape, _mybir.dt.float32, kind="ExternalOutput").ap()
    graph_attention(nc, *args, out)
    r = _run(nc, [arrays], core_ids=[0])
    return r.results[0]["out_dram"]
```
